# Optimizing a Trainium2 kernel written in Bass

```python
import numpy as np
import jax
import jax.numpy as jnp

def _softmax(x, axis=-1):
    return jax.nn.softmax(x, axis=axis)

def _gelu(x):
    return jax.nn.gelu(x, approximate=True)

def _silu(x):
    return jax.nn.silu(x)

def _sigmoid(x):
    return jax.nn.sigmoid(x)

def _layernorm(x, axis=-1, eps=1e-05):
    m = jnp.mean(x, axis=axis, keepdims=True)
    v = jnp.var(x, axis=axis, keepdims=True)
    return (x - m) / jnp.sqrt(v + eps)

def _scatter_add(tgt, idx, src, axis=0):
    return tgt.at[idx].add(src)

def _segment_sum(src, seg, n):
    return jax.ops.segment_sum(src, seg, n)
kernel_name = 'mk_seq_postln_d1_jaxref_r8_44db34'

def setup_inputs(seed: int=0):
    np.random.seed(seed)
    _w = jnp.asarray

    def _L0_attn_setup():
        import jax, jax.numpy as jnp
        import numpy as np
        B, T, H, S, F, G = (2, 256, 512, 128, 1248, 6)
        GRAD_ORDER_MIN = 4
        THD = 2.5
        key = jax.random.key(seed)
        ks = jax.random.split(key, 9)
        sc = 0.02
        hidden_states = jax.random.normal(ks[0], (B, T, H), jnp.float32)
        up_w = jax.random.normal(ks[1], (S, H), jnp.float32) * sc
        gate_w = jax.random.normal(ks[2], (S, H), jnp.float32) / np.sqrt(H)
        local_point = jax.random.normal(ks[3], (S,), jnp.float32)
        local_approx_output = jax.random.normal(ks[4], (H, S), jnp.float32) * sc
        fuse_weight = jax.random.normal(ks[5], (H, S, G), jnp.float32) * sc
        discount_factor = jnp.asarray(np.cumsum(np.log(np.arange(1, G + 1, dtype=np.float64))), jnp.float32)
        ffn_gate_w = jax.random.normal(ks[6], (F, H), jnp.float32) * sc
        ffn_up_w = jax.random.normal(ks[7], (F, H), jnp.float32) * sc
        ffn_down_w = jax.random.normal(ks[8], (H, F), jnp.float32) * sc
        return {'hidden_states': hidden_states, 'up_w': up_w, 'gate_w': gate_w, 'local_point': local_point, 'local_approx_output': local_approx_output, 'fuse_weight': fuse_weight, 'discount_factor': discount_factor, 'ffn_gate_w': ffn_gate_w, 'ffn_up_w': ffn_up_w, 'ffn_down_w': ffn_down_w}
    _L0_attn_in = _L0_attn_setup()

    def _L0_ffn_setup():
        import jax, jax.numpy as jnp
        import numpy as np
        DIM = 512
        INTER = 1792
        SPARSITY = 32
        RANK = 16
        key = jax.random.key(seed)
        ks = jax.random.split(key, 5)
        B, T = (32, 1)
        x = jax.random.normal(ks[0], (B, T, DIM), dtype=jnp.float32)
        c1_w = jax.random.normal(ks[1], (RANK, DIM), dtype=jnp.float32) * (1.0 / np.sqrt(DIM))
        c2_w = jax.random.normal(ks[2], (INTER, RANK), dtype=jnp.float32) * (1.0 / np.sqrt(RANK))
        w1 = jax.random.normal(ks[3], (INTER, DIM), dtype=jnp.float32) * (1.0 / np.sqrt(DIM))
        w2t = jax.random.normal(ks[4], (INTER, DIM), dtype=jnp.float32) * (1.0 / np.sqrt(INTER))
        return {'x': x, 'c1_w': c1_w, 'c2_w': c2_w, 'w1': w1, 'w2t': w2t}
    _L0_ffn_in = _L0_ffn_setup()
    _d = {'L0_attn_hidden_states': _L0_attn_in['hidden_states'], 'L0_attn_up_w': _L0_attn_in['up_w'], 'L0_attn_gate_w': _L0_attn_in['gate_w'], 'L0_attn_local_point': _L0_attn_in['local_point'], 'L0_attn_local_approx_output': _L0_attn_in['local_approx_output'], 'L0_attn_fuse_weight': _L0_attn_in['fuse_weight'], 'L0_attn_discount_factor': _L0_attn_in['discount_factor'], 'L0_attn_ffn_gate_w': _L0_attn_in['ffn_gate_w'], 'L0_attn_ffn_up_w': _L0_attn_in['ffn_up_w'], 'L0_attn_ffn_down_w': _L0_attn_in['ffn_down_w'], 'L0_ffn_c1_w': _L0_ffn_in['c1_w'], 'L0_ffn_c2_w': _L0_ffn_in['c2_w'], 'L0_ffn_w1': _L0_ffn_in['w1'], 'L0_ffn_w2t': _L0_ffn_in['w2t']}
    _x0 = _d['L0_attn_hidden_states']
    _d['L0_attn_hidden_states'] = jax.random.normal(jax.random.fold_in(jax.random.key(seed), 1), (2, 1024, 512), dtype=_x0.dtype)
    del _x0
    return _d

def reference(L0_attn_hidden_states, L0_attn_up_w, L0_attn_gate_w, L0_attn_local_point, L0_attn_local_approx_output, L0_attn_fuse_weight, L0_attn_discount_factor, L0_attn_ffn_gate_w, L0_attn_ffn_up_w, L0_attn_ffn_down_w, L0_ffn_c1_w, L0_ffn_c2_w, L0_ffn_w1, L0_ffn_w2t):

    def _L0_attn_ref(hidden_states, up_w, gate_w, local_point, local_approx_output, fuse_weight, discount_factor, ffn_gate_w, ffn_up_w, ffn_down_w):
        import jax, jax.numpy as jnp
        import numpy as np
        B, T, H, S, F, G = (2, 256, 512, 128, 1248, 6)
        GRAD_ORDER_MIN = 4
        THD = 2.5
        approx_up = hidden_states @ up_w.T
        gate_pre = hidden_states @ gate_w.T
        delta = gate_pre - local_point
        neg_factor = jnp.where(delta > 0, 1.0, -1.0).astype(hidden_states.dtype)
        delta_abs = jnp.abs(delta)
        log_delta = jnp.log(delta_abs)
        keep = (delta_abs <= THD).astype(hidden_states.dtype)
        approx_out = approx_up @ local_approx_output.T
        for idx in range(G):
            m = idx + 1
            dterm = jnp.exp(log_delta * m - discount_factor[idx])
            if m % 2 == 1:
                dterm = dterm * neg_factor
            tmp = dterm * approx_up
            if m > GRAD_ORDER_MIN:
                tmp = tmp * keep
            approx_out = approx_out + tmp @ fuse_weight[:, :, idx].T
        ffn_out = jax.nn.silu(hidden_states @ ffn_gate_w.T) * (hidden_states @ ffn_up_w.T) @ ffn_down_w.T
        return approx_out + ffn_out

    def _L0_ffn_ref(x, c1_w, c2_w, w1, w2t):
        import jax, jax.numpy as jnp
        import numpy as np
        DIM = 512
        INTER = 1792
        SPARSITY = 32
        RANK = 16
        B, T, M = x.shape
        xf = x.reshape(B * T, M)
        inter = xf @ c1_w.T @ c2_w.T
        n_blocks = INTER // SPARSITY
        blk = inter.reshape(B * T, n_blocks, SPARSITY)
        idx = jnp.argmax(blk, axis=-1) + jnp.arange(0, INTER, SPARSITY)
        w1_g = w1[idx]
        w2_g = w2t[idx]
        h = jax.nn.relu(jnp.einsum('bkm,bm->bk', w1_g, xf))
        out = jnp.einsum('bk,bkm->bm', h, w2_g)
        return out.reshape(B, T, M)
    x = L0_attn_hidden_states
    x = _layernorm(x + _L0_attn_ref(x, L0_attn_up_w, L0_attn_gate_w, L0_attn_local_point, L0_attn_local_approx_output, L0_attn_fuse_weight, L0_attn_discount_factor, L0_attn_ffn_gate_w, L0_attn_ffn_up_w, L0_attn_ffn_down_w), axis=-1)
    x = _layernorm(x + _L0_ffn_ref(x, L0_ffn_c1_w, L0_ffn_c2_w, L0_ffn_w1, L0_ffn_w2t), axis=-1)
    return x

_drawn_inputs = setup_inputs


def setup_inputs(seed=0):
    import zlib

    import numpy as np

    out = dict(_drawn_inputs(seed))
    spreads = {}
    factors = {}
    for name, (base, spread) in spreads.items():
        noise = np.random.default_rng([zlib.crc32(name.encode()), seed]).standard_normal(out[name].shape)
        drawn = base * np.exp(spread * noise) if base else spread * noise
        out[name] = jnp.asarray(drawn.astype(out[name].dtype))
    for name, factor in factors.items():
        out[name] = (out[name] * factor).astype(out[name].dtype)
    return out
```

```python
from contextlib import ExitStack, contextmanager

import concourse.bass as bass
from concourse import mybir

F32 = mybir.dt.float32
F16 = mybir.dt.float16
BF16 = mybir.dt.bfloat16
I32 = mybir.dt.int32
U8 = mybir.dt.uint8
ALU = mybir.AluOpType
ACT = mybir.ActivationFunctionType
AX = mybir.AxisListType
ABSMAX = bass.bass_isa.ReduceOp.absmax

P = 128
TOKENS, H, S, G = 2048, 512, 128, 6
F1, F2, RANK, SPARSITY = 1248, 1792, 16, 32
THD, EPS = 2.5, 1e-5
KC = H // P
GT = 512
GROUPS = TOKENS // GT
TPG = GT // P
C1 = -(-F1 // P)
C2 = F2 // P
U1, U2 = C1 // 2, C2 // 2
BLOCKS = F2 // SPARSITY
COPIES = P // RANK
PICK_COLS = 448
PICKS = F2 // PICK_COLS
PB = PICK_COLS // SPARSITY
BPC = P // SPARSITY

W2_SLOT, W1_SLOT = 2 * H, 3 * H
W2_AT = 0
AUX_AT = W2_AT + C2 * W2_SLOT
AUX_WORDS = 2048
W1_AT = AUX_AT + AUX_WORDS
BIG_WORDS = W1_AT + C1 * W1_SLOT
XT_AT = W2_AT
FUSE_AT = XT_AT + 2 * KC * GT
UG_AT = FUSE_AT + (G + 1) * H
TERM_AT = UG_AT + KC * 2 * S
DELTA_AT = TERM_AT + (G + 1) * GT
assert DELTA_AT + 3 * GT <= AUX_AT

TOP = 13
X1_SCALE = 2.0 ** 9
HID_SCALE = 2.0 ** -17
CONST_COLS = 6 + SPARSITY + P

MAX_ORDER = [("x", 0), ("c1", 0), ("x", 1), ("x", 2), ("w", 0), ("w", 1), ("x", 3), ("w", 2), ("w", 3)]


class Steps:

    def __init__(self, engine, sem):
        self.engine, self.sem, self.base, self.n = engine, sem, 0, 0

    def did(self, instruction):
        instruction.then_inc(self.sem, 1)
        self.n += 1

    def settle(self):
        self.engine.wait_ge(self.sem, self.base + self.n)

    @contextmanager
    def loop(self, start, end, per):
        base, n = self.base, self.n
        with self.engine.Fori(start, end) as i:
            self.base, self.n = base + n + (i - start) * per, 0
            yield i
            assert self.n == per, (self.n, per)
        self.base, self.n = base, n + (end - start) * per


def program(nc, x, x_t, ug_t, point, discount, fuse_t, w1_all, c1_rep, c2_rep, w2_all, consts, out):
    ctx = ExitStack()
    with ctx:
        def sb(name, shape, dt):
            return ctx.enter_context(nc.sbuf_tensor(name, shape, dt))

        def sem(name):
            return ctx.enter_context(nc.semaphore(name))

        big = sb("big", [P, 2 * BIG_WORDS], F16)
        big16, big32 = big[:, :], big[:, :].bitcast(F32)
        rows = sb("rows", [P, GROUPS * TPG, H], F32)
        xs = sb("xs", [P, GROUPS * 2 * KC * GT], F16)
        work = sb("work", [P, 2 * 3072], F16)
        work32 = work[:, :].bitcast(F32)
        c2_stack = sb("c2_stack", [P, F2], BF16)
        c1_parts = sb("c1_parts", [P, 2 * KC * P], F16)
        const_sb = sb("const_sb", [P, CONST_COLS], F32)
        ident16 = sb("ident16", [P, P], F16)
        rev16 = sb("rev16", [P, SPARSITY], F16)
        winner = sb("winner", [P, GROUPS * TPG, BLOCKS], U8)
        point_sb = sb("point_sb", [P, 1], F32)
        disc_sb = sb("disc_sb", [P, G], F32)
        sc = sb("sc", [P, 64], F32)
        small = sb("small", [P, 44], F32)

        slice_mask = [const_sb[:, i:i + 1] for i in range(6)]
        ident32 = const_sb[:, 6 + SPARSITY:6 + SPARSITY + P]

        x_part, x_all = sc[:, 0:4], sc[:, 4:8]
        w_part, w_all = sc[:, 8:12], sc[:, 12:16]
        x_exp, x_scale, x_inv = sc[:, 16:20], sc[:, 20:24], sc[:, 24:28]
        w_max, w_exp, w_scale, w_inv = sc[:, 28:30], sc[:, 30:32], sc[:, 32:34], sc[:, 34:36]
        gate_out, up_out, down_out = sc[:, 36:40], sc[:, 40:44], sc[:, 44:48]
        spare, hid_out = sc[:, 48:52], sc[:, 52:53]
        factor = sc[:, 53:53 + G]
        c1_part, c1_all, c1_exp, c1_scale, c1_inv = [sc[:, i:i + 1] for i in range(59, 64)]
        stats = small[:, 0:24].rearrange("p (t s) -> p t s", t=TPG)
        mv = small[:, 24:32].rearrange("p (t s) -> p t s", t=TPG)
        ve, y, ya = small[:, 32:36], small[:, 36:40], small[:, 40:44]

        def words(at, n):
            return big32[:, at:at + n]

        xt = [words(XT_AT + i * KC * GT, KC * GT) for i in range(2)]
        fuse = [words(FUSE_AT + m * H, H) for m in range(G + 1)]
        ug = words(UG_AT, KC * 2 * S)
        term = [words(TERM_AT + m * GT, GT) for m in range(G + 1)]
        delta, keep, delta_keep = [words(DELTA_AT + i * GT, GT) for i in range(3)]

        w1_raw = words(W1_AT - W1_SLOT, C1 * W1_SLOT)
        w2_raw = words(W2_AT + W2_SLOT, C2 * W2_SLOT)

        def w1_part(s, k, part):
            at = 2 * W1_AT + k * 2 * H + part * H
            return lambda a, n: big16[:, bass.ds(s * (2 * W1_SLOT) + (at + a), n)]

        def w2_part(c, k, part):
            at = 2 * W2_AT + k * 2 * H + part * H
            return lambda a, n: big16[:, bass.ds(c * (2 * W2_SLOT) + (at + a), n)]

        def x_part16(g, part, kc, a=0, n=GT):
            return xs[:, bass.ds(g * (2 * KC * GT) + ((part * KC + kc) * GT + a), n)]

        act32 = [work32[:, j * GT:(j + 1) * GT] for j in range(2)]

        def act_part(pair, j, part, a=0, n=GT):
            return work[:, bass.ds((pair % 2) * (4 * GT) + (4 * GT + (2 * j + part) * GT + a), n)]

        c2_raw = work32[:, 0:F2]
        c2_round = work[:, 2 * F2:3 * F2].bitcast(BF16)
        assert 3 * F2 <= 6144
        c1_raw = xs[:, (GROUPS - 1) * 2 * KC * GT:(GROUPS - 1) * 2 * KC * GT + 2 * KC * P].bitcast(F32)

        a32 = AUX_AT
        x1_part = [big16[:, 2 * a32 + i * H:2 * a32 + (i + 1) * H] for i in range(2)]
        a16 = 2 * (a32 + H)
        z_rest = words(a32 + H, P)
        z_hi = big16[:, a16 + 256:a16 + 384].bitcast(BF16)
        z_mid = big16[:, a16 + 384:a16 + 512].bitcast(BF16)
        z_stack = big16[:, a16 + 512:a16 + 640].bitcast(BF16)
        hit = [big16[:, a16 + 640 + i * PICK_COLS:a16 + 640 + (i + 1) * PICK_COLS] for i in range(2)]
        rank = [big16[:, a16 + 1536 + i * PICK_COLS:a16 + 1536 + (i + 1) * PICK_COLS] for i in range(2)]
        block_max = [words(a32 + H + 1216 + i * 16, PB) for i in range(2)]
        assert a32 + H + 1248 <= W1_AT
        mask_at = 2 * (W1_AT + 5 * W1_SLOT)
        mask = big16[:, mask_at:mask_at + TPG * 2 * P]

        def bank(name):
            return ctx.enter_context(nc.psum_tensor(name, [P, 512], F32))

        pa, pb, pick_a, pick_b = bank("pa"), bank("pb"), bank("pick_a"), bank("pick_b")
        acc = [bank(f"acc{t}") for t in range(TPG)]
        pick_bank = [pick_a, pick_b]

        ug_in, fuse_in, small_in, c2_in = sem("ug_in"), sem("fuse_in"), sem("small_in"), sem("c2_in")
        xt_in = [sem("xt_in0"), sem("xt_in1")]
        rows_in = [sem(f"rows_in{g}") for g in range(GROUPS)]
        w1_in = [sem("w1_in0"), sem("w1_in1")]
        w2_in = [sem("w2_in0"), sem("w2_in1")]
        out_done = sem("out_done")
        u_ready, delta_pre_ready, taylor_ready = sem("u_ready"), sem("delta_pre_ready"), sem("taylor_ready")
        gate_ready, up_ready, down_ready = sem("gate_ready"), sem("up_ready"), sem("down_ready")
        x1t_ready, z_ready, score_ready = sem("x1t_ready"), sem("z_ready"), sem("score_ready")
        mask_t_ready, hid_ready, sparse_ready = sem("mask_t_ready"), sem("hid_ready"), sem("sparse_ready")
        factor_ready, fuse_scaled, u_copied, xhi_ready = sem("factor_ready"), sem("fuse_scaled"), sem("u_copied"), sem("xhi_ready")
        silu_ready, act_hi = sem("silu_ready"), sem("act_hi")
        w1_hi, w2_hi = sem("w1_hi"), sem("w2_hi")
        x1_hi, x1t_copied, relu_ready, c1_hi = sem("x1_hi"), sem("x1t_copied"), sem("relu_ready"), sem("c1_hi")
        act_lo, max_ready = sem("act_lo"), sem("max_ready")
        vstep = sem("vstep")
        delta_ready, terms_ready, banks_added = sem("delta_ready"), sem("terms_ready"), sem("banks_added")
        max_part, x_scaled, w_scaled, xlo_ready = sem("max_part"), sem("x_scaled"), sem("w_scaled"), sem("xlo_ready")
        w1_lo, w2_lo, swiglu_ready = sem("w1_lo"), sem("w2_lo"), sem("swiglu_ready")
        x1_ready, x1_lo, z_stacked, score_used = sem("x1_ready"), sem("x1_lo"), sem("z_stacked"), sem("score_used")
        c1_scaled, c1_lo = sem("c1_scaled"), sem("c1_lo")
        c2_stacked, mask_ready, masked, rows_out = sem("c2_stacked"), sem("mask_ready"), sem("masked"), sem("rows_out")

        N1 = GROUPS * C1
        def added(phase, g, t):
            return TPG * (1 + GROUPS * phase) + TPG * g + (t + 1)

        act_passed, vector_passed, tensor_passed = sem("act_passed"), sem("vector_passed"), sem("tensor_passed")

        def apart(engine, passed):
            engine.sem_inc(passed, 1)

        block = ctx.enter_context(nc.Block())

        @block.sync
        def _(sp):
            sp.dma_start(ug, ug_t).then_inc(ug_in, 16)

            def load_xt(g):
                sp.dma_start(xt[g % 2].rearrange("p (k t) -> p k t", k=KC),
                             x_t[:, :, g * GT:(g + 1) * GT]).then_inc(xt_in[g % 2], 16)

            def load_rows(g):
                sp.dma_start(rows[:, g * TPG:(g + 1) * TPG, :],
                             x[g * GT:(g + 1) * GT, :].rearrange("(t p) m -> p t m", p=P)).then_inc(rows_in[g], 16)

            load_xt(0)
            for dst, src in ((point_sb[:, :], point), (disc_sb[:, :], discount), (const_sb[:, :], consts), (c1_raw, c1_rep)):
                sp.dma_start(dst, src).then_inc(small_in, 16)
            sp.dma_start(words(FUSE_AT, (G + 1) * H), fuse_t).then_inc(fuse_in, 16)
            load_xt(1)
            load_rows(0)
            sp.dma_start(c2_raw, c2_rep).then_inc(c2_in, 16)
            half = C1 // 2 * W1_SLOT
            for i in range(2):
                sp.dma_start(w1_raw[:, i * half:(i + 1) * half], w1_all[:, i * half:(i + 1) * half]).then_inc(w1_in[i], 16)
                load_rows(1 + i)
                g = 2 + i
                sp.wait_ge(delta_pre_ready, g - 1)
                sp.wait_ge(xlo_ready, g - 1)
                load_xt(g)
            load_rows(3)
            sp.wait_ge(taylor_ready, GROUPS * TPG)
            sp.wait_ge(xlo_ready, GROUPS)
            sp.wait_ge(w1_lo, 3 * C1)
            half = C2 // 2 * W2_SLOT
            for i in range(2):
                sp.dma_start(w2_raw[:, i * half:(i + 1) * half], w2_all[:, i * half:(i + 1) * half]).then_inc(w2_in[i], 16)
            for g in range(GROUPS):
                sp.wait_ge(rows_out, TPG * (g + 1))
                sp.dma_start(out[g * GT:(g + 1) * GT, :].rearrange("(t p) m -> p t m", p=P),
                             rows[:, g * TPG:(g + 1) * TPG, :]).then_inc(out_done, 16)
            sp.wait_ge(out_done, 16 * GROUPS)

        @block.tensor
        def _(pe):
            def split_product(dst, weights, g):
                apart(pe, tensor_passed)
                for kc in range(KC):
                    for wp, xp in ((0, 0), (0, 1), (1, 0)):
                        mm = nc.tensor.matmul(dst[:, :], weights(wp)(kc * P, P), x_part16(g, xp, kc),
                                              start=(kc == 0 and wp == xp), stop=(kc == KC - 1 and wp == 1))
                return mm

            def second_product(pair, j, weights, first, last, done=None, free=None):
                for t in range(TPG):
                    if free is not None:
                        pe.wait_ge(banks_added, free(t))
                    if t == 0 or free is not None:
                        apart(pe, tensor_passed)
                    for ap, wp in ((0, 0), (0, 1), (1, 0)):
                        mm = nc.tensor.matmul(acc[t][:, :], act_part(pair, j, ap, t * P, P), weights(wp)(0, H),
                                              start=(first and ap == wp), stop=(last and ap == 1))
                    if done is not None:
                        mm.then_inc(done, 1)

            pe.wait_ge(ug_in, 16)
            ug_v = ug.rearrange("p (k s) -> p k s", k=KC)
            with pe.Fori(0, GROUPS // 2) as h:
                for i in range(2):
                    g = h * 2 + i
                    pe.wait_ge(xt_in[i], h * 16 + 16)
                    for dst, col, done in ((pa, 0, u_ready), (pb, S, delta_pre_ready)):
                        for kc in range(KC):
                            mm = nc.tensor.matmul(dst[:, :], ug_v[:, kc, col:col + S], xt[i][:, kc * GT:(kc + 1) * GT],
                                                  start=(kc == 0), stop=(kc == KC - 1))
                        mm.then_inc(done, 1)
                    for m in range(G + 1):
                        if m == 0:
                            pe.wait_ge(u_copied, g + 1)
                            pe.wait_ge(fuse_scaled, G)
                            pe.wait_ge(banks_added, g * TPG + TPG)
                        else:
                            pe.wait_ge(terms_ready, g * G + m)
                        for t in range(TPG):
                            mm = nc.tensor.matmul(acc[t][:, :], term[m][:, t * P:(t + 1) * P], fuse[m],
                                                  start=(m == 0), stop=(m == G))
                            if m == G:
                                mm.then_inc(taylor_ready, 1)

            def transposes(tile, dst, free):
                pe.wait_ge(x1_lo, tile + 1)
                pe.wait_ge(score_used, free)
                for part in range(2):
                    for kc in range(KC):
                        mm = nc.tensor.transpose(dst[:, :].bitcast(F16)[:, part * H + kc * P:part * H + (kc + 1) * P],
                                                 x1_part[part][:, kc * P:(kc + 1) * P], ident16[:, :])
                mm.then_inc(x1t_ready, 1)

            def z_product(tile, g, t, dst, free):
                pe.wait_ge(score_used, free)
                pe.wait_ge(x1t_copied, tile + 1)
                for kc in range(KC):
                    for wp, xp in ((0, 0), (0, 1), (1, 0)):
                        mm = nc.tensor.matmul(dst[:, 0:P], c1_parts[:, (wp * KC + kc) * P:(wp * KC + kc + 1) * P],
                                              x_part16(g, xp, kc, t * P, P),
                                              start=(kc == 0 and wp == xp), stop=(kc == KC - 1 and wp == 1))
                mm.then_inc(z_ready, 1)

            def scores(tile, k, dst):
                pe.wait_ge(z_stacked, tile + 1)
                nc.tensor.matmul(dst[:, 0:PICK_COLS], z_stack, c2_stack[:, k * PICK_COLS:(k + 1) * PICK_COLS],
                                 start=True, stop=True).then_inc(score_ready, 1)

            def unit1(g, u, tile=None, start=False):
                for j in range(2):
                    n = g * C1 + u * 2 + j
                    s = (C1 - 1 - j) - u * 2
                    if not (start and j == 0):
                        pe.wait_ge(silu_ready, n)
                    split_product(pa, lambda part: w1_part(s, 0, part), g).then_inc(gate_ready, 1)
                    if tile is not None:
                        if j == 0:
                            transposes(tile, pick_a, tile * PICKS + 3)
                        else:
                            scores(tile, 0, pick_a)
                    if not (start and j == 0):
                        pe.wait_ge(swiglu_ready, n)
                    split_product(pb, lambda part: w1_part(s, 1, part), g).then_inc(up_ready, 1)
                    if tile is not None:
                        if j == 0:
                            z_product(tile, g - 1, u - 1, pick_b, tile * PICKS + 4)
                        else:
                            scores(tile, 1, pick_b)
                            pe.wait_ge(score_used, tile * PICKS + 5)
                            scores(tile, 2, pick_a)

            def down(g, u, kind, tile=None):
                before = g * U1 + u - 1
                for j in range(2):
                    m = before * 2 + j
                    slot = (C1 - 1 - j) - (u - 1) * 2 if kind != "last" else C1 - 1 - (C1 - 2 + j)
                    pe.wait_ge(act_lo, m + 1)
                    first, last = kind == "first" and j == 0, kind == "last" and j == 1
                    second_product(before, j, lambda part: w1_part(slot, 2, part), first, last,
                                   done=down_ready if last else None,
                                   free=(lambda t: added(1, g - 1, t)) if first else None)
                    if tile is not None and j == 0:
                        pe.wait_ge(score_used, tile * PICKS + 6)
                        scores(tile, 3, pick_b)

            def full_unit1(g, u, kind, tile):
                unit1(g, u, tile)
                down(g, u, kind, tile)

            pe.wait_ge(xlo_ready, GROUPS)
            pe.wait_ge(c1_lo, 1)
            pe.wait_ge(c2_stacked, 1)
            pe.wait_ge(banks_added, added(0, GROUPS - 1, TPG - 1))
            pe.wait_ge(w1_lo, 3 * 2)
            pe.wait_ge(u_copied, GROUPS)
            pe.wait_ge(delta_ready, GROUPS)
            unit1(0, 0, start=True)
            pe.wait_ge(w1_lo, 3 * C1)
            for start, end in ((0, 1), (1, GROUPS - 1), (GROUPS - 1, GROUPS)):
                with pe.Fori(start, end) as g:
                    tile = (lambda u: (g - 1) * TPG + (u - 1)) if start else (lambda u: None)
                    full_unit1(g, 1, "first", tile(1))
                    with pe.Fori(2, U1) as u:
                        full_unit1(g, u, "middle", tile(u))
                    if end < GROUPS:
                        unit1(g + 1, 0)
                        down(g + 1, 0, "last")

            def second2(g, u, kind):
                before = g * U2 + u - 1
                for j in range(2):
                    c = (u - 1) * 2 + j if kind != "last" else C2 - 2 + j
                    pe.wait_ge(act_lo, N1 + before * 2 + j + 1)
                    first, last = kind == "first" and j == 0, kind == "last" and j == 1
                    second_product(before + GROUPS * U1, j, lambda part: w2_part(c, 1, part), first, last,
                                   done=sparse_ready if last else None,
                                   free=(lambda t: added(2, g - 1, t)) if first else None)

            def mask_transposes(unit):
                pe.wait_ge(mask_ready, unit + 1)
                dst = pick_a[:, :].bitcast(F16)
                for j in range(2):
                    for t in range(TPG):
                        mm = nc.tensor.transpose(dst[:, j * GT + t * P:j * GT + (t + 1) * P],
                                                 mask[:, (t * 2 + j) * P:(t * 2 + j + 1) * P], ident16[:, :])
                mm.then_inc(mask_t_ready, 1)

            def unit2(g, u, tile=None, step=None, start=False):
                if tile is not None:
                    if step == 1:
                        scores(tile, 0, pick_b)
                    elif step == 2:
                        pe.wait_ge(score_used, tile * PICKS + 6)
                        scores(tile, 2, pick_b)
                for j, dst in enumerate((pa, pb)):
                    n = g * C2 + u * 2 + j
                    if not start:
                        pe.wait_ge(relu_ready, n - 1)
                    split_product(dst, lambda part: w2_part(u * 2 + j, 0, part), g).then_inc(hid_ready, 1)
                    if j == 0:
                        if not start:
                            pe.wait_ge(masked, n)
                        mask_transposes(g * U2 + u)
                        if step == 0:
                            transposes(tile, pick_b, tile * PICKS + 4)
                if tile is not None:
                    if step == 0:
                        z_product(tile, GROUPS - 1, tile - (GROUPS - 1) * TPG, pick_b, tile * PICKS + 4)
                    elif step == 1:
                        pe.wait_ge(score_used, tile * PICKS + 5)
                        scores(tile, 1, pick_b)
                    else:
                        pe.wait_ge(score_used, tile * PICKS + 7)
                        scores(tile, 3, pick_b)

            pe.wait_ge(w2_lo, 2 * C2 + 2)
            pe.wait_ge(silu_ready, N1)
            pe.wait_ge(swiglu_ready, N1)
            pe.wait_ge(score_used, PICKS + (GROUPS - 1) * TPG * PICKS)
            unit2(0, 0, start=True)
            down(GROUPS, 0, "last")

            def group2(g, picks):
                tile0 = (GROUPS - 1) * TPG + g * 2
                if picks:
                    for u in range(1, U2):
                        unit2(g, u, tile0 + (u - 1) // 3, (u - 1) % 3)
                        second2(g, u, "first" if u == 1 else "middle")
                else:
                    unit2(g, 1)
                    second2(g, 1, "first")
                    with pe.Fori(2, U2) as u:
                        unit2(g, u)
                        second2(g, u, "middle")

            with pe.Fori(0, 2) as g:
                group2(g, True)
                unit2(g + 1, 0)
                second2(g + 1, 0, "last")
            group2(2, False)
            unit2(3, 0)
            second2(3, 0, "last")
            group2(3, False)
            second2(GROUPS, 0, "last")

        @block.scalar
        def _(act):
            act.wait_ge(small_in, 16 * 4)
            act.activation(factor, disc_sb[:, :], ACT.Exp, scale=-1.0).then_inc(factor_ready, 1)
            act.wait_ge(fuse_in, 16)
            act.wait_ge(factor_ready, 1)
            for m in range(1, G + 1):
                act.activation(fuse[m], fuse[m], ACT.Copy, scale=factor[:, m - 1:m]).then_inc(fuse_scaled, 1)

            def x_hi(g, i):
                act.wait_ge(x_scaled, g + 1)
                act.activation(xs[:, bass.ds(g * (2 * KC * GT), KC * GT)], xt[i], ACT.Copy,
                               scale=x_scale[:, bass.ds(g, 1)]).then_inc(xhi_ready, 1)

            for g in range(GROUPS):
                act.wait_ge(u_ready, g + 1)
                act.activation(term[0], pa[:, :], ACT.Copy).then_inc(u_copied, 1)
                x_hi(g, g % 2)
                if g == 0:
                    act.wait_ge(c1_scaled, 1)
                    act.activation(c1_parts[:, 0:KC * P], c1_raw, ACT.Copy, scale=c1_scale).then_inc(c1_hi, 1)

            act.wait_ge(w_scaled, 1)
            for d in range(C1):
                s = C1 - 1 - d
                for k in range(3):
                    if d:
                        act.wait_ge(w1_lo, 3 * (d - 1) + k + 1)
                    act.activation(w1_part(s, k, 0)(0, H), w1_raw[:, s * W1_SLOT + k * H:s * W1_SLOT + (k + 1) * H],
                                   ACT.Copy, scale=w_scale[:, 0:1]).then_inc(w1_hi, 1)

            def swiglu(g, u, start=False, tile=None):
                pair = g * U1 + u
                if tile is not None:
                    x1_high(tile)
                for j in range(2):
                    n = g * C1 + u * 2 + j
                    act.wait_ge(gate_ready, n + 1)
                    if not start:
                        act.wait_ge(act_lo, n - 1)
                    apart(act, act_passed)
                    act.activation(act32[j], pa[:, :], ACT.Silu, scale=gate_out[:, bass.ds(g, 1)]).then_inc(silu_ready, 1)
                    if tile is not None and j == 0:
                        x1t_copy(g - 1, u - 1, pick_a)
                    act.wait_ge(swiglu_ready, n + 1)
                    apart(act, act_passed)
                    act.activation(act_part(pair, j, 0), act32[j], ACT.Copy).then_inc(act_hi, 1)

            def x1_high(tile):
                act.wait_ge(x1_ready, tile + 1)
                apart(act, act_passed)
                act.activation(x1_part[0], rows[:, bass.ds(tile, 1), :].rearrange("p a m -> p (a m)"), ACT.Copy,
                               scale=X1_SCALE).then_inc(x1_hi, 1)

            def x1t_copy(g, t, src):
                act.wait_ge(x1t_ready, g * TPG + (t + 1))
                apart(act, act_passed)
                dst = xs[:, bass.ds(g * (2 * KC * GT), 2 * KC * GT)].rearrange("p (k t) -> p k t", k=2 * KC)
                act.activation(dst[:, :, bass.ds(t * P, P)], src[:, :].bitcast(F16).rearrange("p (k t) -> p k t", k=2 * KC),
                               ACT.Copy).then_inc(x1t_copied, 1)

            def w2_high(i):
                act.wait_ge(w_scaled, 2)
                half = C2 // 2
                with act.Fori(i * half, (i + 1) * half) as c:
                    for k in range(2):
                        act.wait_ge(w2_lo, c * 2 + (k + 1))
                        apart(act, act_passed)
                        act.activation(w2_part(c, k, 0)(0, H), big32[:, bass.ds(c * W2_SLOT + (W2_AT + W2_SLOT + k * H), H)],
                                       ACT.Copy, scale=w_scale[:, 1:2]).then_inc(w2_hi, 1)

            swiglu(0, 0, start=True)
            with act.Fori(1, 3) as u:
                swiglu(0, u)
            swiglu(0, 3)
            w2_high(0)
            swiglu(0, 4)
            w2_high(1)
            act.wait_ge(w2_lo, 2 * C2 + 2)
            with act.Fori(1, GROUPS) as g:
                swiglu(g, 0)
                with act.Fori(1, U1) as u:
                    swiglu(g, u, tile=g * TPG + u - (TPG + 1))

            def hidden(g, u, t=None):
                if t is not None:
                    x1_high(t + (GROUPS - 1) * TPG)
                for j in range(2):
                    n = g * C2 + u * 2 + j
                    act.wait_ge(hid_ready, n + 1)
                    act.wait_ge(act_lo, N1 + n - 1)
                    apart(act, act_passed)
                    act.activation(act32[j], (pa, pb)[j][:, :], ACT.Relu, scale=HID_SCALE).then_inc(relu_ready, 1)
                    act.wait_ge(masked, n + 1)
                    apart(act, act_passed)
                    act.activation(act_part(GROUPS * U1 + g * U2 + u, j, 0), act32[j], ACT.Copy).then_inc(act_hi, 1)
                    if t is not None and j == 0:
                        x1t_copy(GROUPS - 1, t, pick_b)

            with act.Fori(0, 2) as g:
                hidden(g, 0)
                with act.Fori(0, 2) as i:
                    for step in range(3):
                        hidden(g, i * 3 + (1 + step), g * 2 + i if step == 0 else None)
            with act.Fori(2, GROUPS) as g:
                with act.Fori(0, U2) as u:
                    hidden(g, u)

        @block.gpsimd
        def _(pool):
            def reduce_max(i):
                what, col = MAX_ORDER[i]
                part, whole = {"x": (x_part, x_all), "w": (w_part, w_all), "c1": (c1_part, c1_all)}[what]
                pool.wait_ge(max_part, i + 1)
                nc.gpsimd.partition_all_reduce(whole[:, col:col + 1], part[:, col:col + 1], P, ABSMAX).then_inc(max_ready, 1)

            def low(pair, j, n):
                pool.wait_ge(act_hi, n + 1)
                nc.gpsimd.tensor_tensor(act_part(pair, j, 1), act32[j], act_part(pair, j, 0), ALU.subtract).then_inc(act_lo, 1)

            for i in range(7):
                reduce_max(i)
            with pool.Fori(0, 3) as u:
                for j in range(2):
                    low(u, j, u * 2 + j)
            for i in range(7, 9):
                reduce_max(i)
            with pool.Fori(3, GROUPS * (U1 + U2)) as u:
                for j in range(2):
                    low(u, j, u * 2 + j)

        @block.vector
        def _(dve):
            v = nc.vector
            steps = Steps(dve, vstep)
            step, settle = steps.did, steps.settle
            dve.sem_inc(banks_added, TPG)
            dve.sem_inc(score_used, PICKS)
            dve.sem_inc(w2_lo, 2)

            def power_scales(m, e, s, inv, signal):
                m, e, s, inv = (a.bitcast(I32) for a in (m, e, s, inv))
                step(v.tensor_scalar(e, m, 0x7F800000, None, ALU.bitwise_and))
                settle()
                step(v.tensor_scalar(e, e, float((127 - 40) << 23), float((127 + 40) << 23), ALU.max, ALU.min))
                settle()
                step(v.tensor_scalar(inv, e, float(-(TOP << 23)), None, ALU.add))
                v.tensor_scalar(s, e, -1.0, float((254 + TOP) << 23), ALU.mult, ALU.add).then_inc(signal, 1)

            def take_tile(tile, t, scalar):
                r = rows[:, bass.ds(tile, 1), :].rearrange("p a m -> p (a m)")
                v.scalar_tensor_tensor(out=r, in0=acc[t][:, :], scalar=scalar, in1=r,
                                       op0=ALU.mult, op1=ALU.add).then_inc(banks_added, 1)

            dve.wait_ge(small_in, 16 * 4)
            step(v.tensor_copy(ident16[:, :], ident32))
            step(v.tensor_copy(rev16[:, :], const_sb[:, 6:6 + SPARSITY]))

            def stack_c2():
                dve.wait_ge(c2_in, 16)
                for i in range(3):
                    step(v.tensor_copy(c2_round, c2_raw))
                    settle()
                    if i == 0:
                        step(v.tensor_scalar(c2_stack[:, :], c2_round, slice_mask[3], None, ALU.mult))
                    else:
                        ins = v.scalar_tensor_tensor(out=c2_stack[:, :], in0=c2_round, scalar=slice_mask[3 + i],
                                                     in1=c2_stack[:, :], op0=ALU.mult, op1=ALU.add)
                        step(ins) if i == 1 else ins.then_inc(c2_stacked, 1)
                    if i < 2:
                        step(v.tensor_tensor(c2_raw, c2_raw, c2_round, ALU.subtract))
                        settle()
                dve.wait_ge(c2_stacked, 1)

            def weights_max(i, src, halves, col):
                dve.wait_ge(halves[i], 16)
                half = src.shape[1] // 2
                v.tensor_reduce(w_part[:, col:col + 1], src[:, i * half:(i + 1) * half], axis=AX.X, op=ALU.max,
                                apply_absolute_value=True).then_inc(max_part, 1)

            def w1_low(d0, d1):
                for d in range(d0, d1):
                    s = C1 - 1 - d
                    for k in range(3):
                        dve.wait_ge(w1_hi, 3 * d + k + 1)
                        v.scalar_tensor_tensor(out=w1_part(s, k, 1)(0, H), in0=w1_raw[:, s * W1_SLOT + k * H:s * W1_SLOT + (k + 1) * H],
                                               scalar=w_scale[:, 0:1], in1=w1_part(s, k, 0)(0, H),
                                               op0=ALU.mult, op1=ALU.subtract).then_inc(w1_lo, 1)

            def scale_phase1():
                step(v.tensor_tensor(w_max[:, 0:1], w_all[:, 0:1], w_all[:, 1:2], ALU.max))
                settle()
                power_scales(w_max[:, 0:1], w_exp[:, 0:1], w_scale[:, 0:1], w_inv[:, 0:1], w_scaled)
                dve.wait_ge(w_scaled, 1)
                settle()
                step(v.tensor_scalar(gate_out, x_inv, w_inv[:, 0:1], None, ALU.mult))
                step(v.tensor_scalar(up_out, x_scale, w_scale[:, 0:1], 2.0 ** -59, ALU.mult, ALU.mult))
                settle()
                step(v.scalar_tensor_tensor(out=spare, in0=gate_out, scalar=2.0 ** 59, in1=gate_out, op0=ALU.mult, op1=ALU.mult))
                settle()
                step(v.tensor_scalar(down_out, spare, w_inv[:, 0:1], None, ALU.mult))
                settle()

            for g in range(GROUPS):
                i = g % 2
                dve.wait_ge(xt_in[i], 16 * (g // 2 + 1))
                v.tensor_reduce(x_part[:, g:g + 1], xt[i], axis=AX.X, op=ALU.max,
                                apply_absolute_value=True).then_inc(max_part, 1)
                dve.wait_ge(delta_pre_ready, g + 1)
                v.tensor_scalar(delta, pb[:, :], point_sb[:, 0:1], None, ALU.subtract).then_inc(delta_ready, 1)
                dve.wait_ge(max_ready, MAX_ORDER.index(("x", g)) + 1)
                power_scales(x_all[:, g:g + 1], x_exp[:, g:g + 1], x_scale[:, g:g + 1], x_inv[:, g:g + 1], x_scaled)
                dve.wait_ge(delta_ready, g + 1)
                dve.wait_ge(u_copied, g + 1)
                v.tensor_tensor(term[1], term[0], delta, ALU.mult).then_inc(terms_ready, 1)
                step(v.scalar_tensor_tensor(out=keep, in0=delta, scalar=-THD, in1=delta, op0=ALU.is_ge, op1=ALU.mult))
                settle()
                step(v.scalar_tensor_tensor(out=delta_keep, in0=delta, scalar=THD, in1=keep, op0=ALU.is_le, op1=ALU.mult))
                for m in range(2, G + 1):
                    dve.wait_ge(terms_ready, g * G + m - 1)
                    if m == 5:
                        settle()
                    v.tensor_tensor(term[m], term[m - 1], delta_keep if m == 5 else delta, ALU.mult).then_inc(terms_ready, 1)
                dve.wait_ge(xhi_ready, g + 1)
                lo = xs[:, ((g * 2 + 1) * KC) * GT:((g * 2 + 2) * KC) * GT]
                hi = xs[:, (g * 2 * KC) * GT:((g * 2 + 1) * KC) * GT]
                v.scalar_tensor_tensor(out=lo, in0=xt[i], scalar=x_scale[:, g:g + 1], in1=hi,
                                       op0=ALU.mult, op1=ALU.subtract).then_inc(xlo_ready, 1)
                if g == 0:
                    v.tensor_reduce(c1_part, c1_raw, axis=AX.X, op=ALU.max, apply_absolute_value=True).then_inc(max_part, 1)
                    dve.wait_ge(max_ready, 2)
                    power_scales(c1_all, c1_exp, c1_scale, c1_inv, c1_scaled)
                    dve.wait_ge(c1_hi, 1)
                    v.scalar_tensor_tensor(out=c1_parts[:, KC * P:2 * KC * P], in0=c1_raw, scalar=c1_scale,
                                           in1=c1_parts[:, 0:KC * P], op0=ALU.mult, op1=ALU.subtract).then_inc(c1_lo, 1)
                if g == 1:
                    stack_c2()
                if g == 2:
                    for half in range(2):
                        weights_max(half, w1_raw, w1_in, half)
                if g == 3:
                    scale_phase1()
                    w1_low(0, 6)
                dve.wait_ge(rows_in[g], 16)
                for t in range(TPG):
                    dve.wait_ge(taylor_ready, g * TPG + t + 1)
                    take_tile(g * TPG + t, t, 1.0)

            w1_low(6, C1)

            def swiglu(g, u, j):
                n = g * C1 + u * 2 + j
                dve.wait_ge(up_ready, n + 1)
                dve.wait_ge(silu_ready, n + 1)
                v.scalar_tensor_tensor(out=act32[j], in0=pb[:, :], scalar=up_out[:, bass.ds(g, 1)], in1=act32[j],
                                       op0=ALU.mult, op1=ALU.mult).then_inc(swiglu_ready, 1)

            def normalise(g, ready, phase, scalar, signal):
                for t in range(TPG):
                    dve.wait_ge(ready, g * TPG + (t + 1))
                    take_tile(g * TPG + t, t, scalar)
                for t in range(TPG):
                    r = rows[:, bass.ds(g * TPG + t, 1), :].rearrange("p a m -> p (a m)")
                    dve.wait_ge(banks_added, added(phase, g, t))
                    apart(dve, vector_passed)
                    step(v.bn_stats(stats[:, t, :], r))
                settle()
                apart(dve, vector_passed)
                for t in range(TPG):
                    step(v.bn_aggr(mv[:, t, :], stats[:, t, :]))
                settle()
                step(v.tensor_scalar(ve, mv[:, :, 1], EPS, None, ALU.add))
                settle()
                step(v.tensor_scalar(ya.bitcast(I32), ve.bitcast(I32), 1, None, ALU.logical_shift_right))
                settle()
                step(v.tensor_scalar(y.bitcast(I32), ya.bitcast(I32), -1.0, float(0x5F3759DF), ALU.mult, ALU.add))
                settle()
                for _ in range(4):
                    step(v.tensor_tensor(ya, y, y, ALU.mult))
                    settle()
                    step(v.tensor_tensor(ya, ya, ve, ALU.mult))
                    settle()
                    step(v.tensor_scalar(ya, ya, -0.5, 1.5, ALU.mult, ALU.add))
                    settle()
                    step(v.tensor_tensor(y, y, ya, ALU.mult))
                    settle()
                for t in range(TPG):
                    r = rows[:, bass.ds(g * TPG + t, 1), :].rearrange("p a m -> p (a m)")
                    v.tensor_scalar(r, r, mv[:, t, 0:1], y[:, t:t + 1], ALU.subtract, ALU.mult).then_inc(signal, 1)

            NORM_STEPS = 4 + 4 + 1 + 2 + 16

            def x1_low(tile):
                dve.wait_ge(x1_hi, tile + 1)
                v.scalar_tensor_tensor(out=x1_part[1], in0=rows[:, bass.ds(tile, 1), :].rearrange("p a m -> p (a m)"),
                                       scalar=X1_SCALE, in1=x1_part[0], op0=ALU.mult, op1=ALU.subtract).then_inc(x1_lo, 1)

            def stack_z(tile, src):
                dve.wait_ge(z_ready, tile + 1)
                z = src[:, 0:P]
                step(v.tensor_copy(z_hi, z))
                settle()
                step(v.tensor_tensor(z_rest, z, z_hi, ALU.subtract))
                settle()
                step(v.tensor_copy(z_mid, z_rest))
                settle()
                step(v.tensor_tensor(z_rest, z_rest, z_mid, ALU.subtract))
                settle()
                step(v.tensor_scalar(z_stack, z_rest, slice_mask[2], None, ALU.mult))
                settle()
                step(v.scalar_tensor_tensor(out=z_stack, in0=z_mid, scalar=slice_mask[1], in1=z_stack, op0=ALU.mult, op1=ALU.add))
                settle()
                v.scalar_tensor_tensor(out=z_stack, in0=z_hi, scalar=slice_mask[0], in1=z_stack,
                                       op0=ALU.mult, op1=ALU.add).then_inc(z_stacked, 1)

            Z_STEPS, PICK_STEPS = 6, 3

            def pick(tile, k, src):
                q = tile * PICKS + k
                b = k % 2
                s = src[:, 0:PICK_COLS].rearrange("p (b j) -> p b j", j=SPARSITY)
                h = hit[b].rearrange("p (b j) -> p b j", j=SPARSITY)
                r = rank[b].rearrange("p (b j) -> p b j", j=SPARSITY)
                dve.wait_ge(score_ready, q + 1)
                step(v.tensor_reduce(block_max[b], s, axis=AX.X, op=ALU.max))
                settle()
                v.tensor_tensor(h, s, block_max[b].unsqueeze(2).broadcast_to([P, PB, SPARSITY]), ALU.is_equal).then_inc(score_used, 1)
                dve.wait_ge(score_used, PICKS + q + 1)
                step(v.tensor_tensor(r, h, rev16[:, :].unsqueeze(1).broadcast_to([P, PB, SPARSITY]), ALU.mult))
                settle()
                step(v.tensor_reduce(winner[:, bass.ds(tile, 1), k * PB:(k + 1) * PB].rearrange("p a b -> p (a b)"), r,
                                     axis=AX.X, op=ALU.max))

            def w2_low(i):
                dve.wait_ge(w_scaled, 2)
                half = C2 // 2
                with dve.Fori(i * half, (i + 1) * half) as c:
                    for k in range(2):
                        dve.wait_ge(w2_hi, c * 2 + (k + 1))
                        v.scalar_tensor_tensor(out=w2_part(c, k, 1)(0, H), in0=big32[:, bass.ds(c * W2_SLOT + (W2_AT + W2_SLOT + k * H), H)],
                                               scalar=w_scale[:, 1:2], in1=w2_part(c, k, 0)(0, H),
                                               op0=ALU.mult, op1=ALU.subtract).then_inc(w2_lo, 1)

            for u in range(3):
                for j in range(2):
                    swiglu(0, u, j)
                if u:
                    weights_max(u - 1, w2_raw, w2_in, 1 + u)
            dve.wait_ge(max_ready, len(MAX_ORDER))
            step(v.tensor_tensor(w_max[:, 1:2], w_all[:, 2:3], w_all[:, 3:4], ALU.max))
            settle()
            power_scales(w_max[:, 1:2], w_exp[:, 1:2], w_scale[:, 1:2], w_inv[:, 1:2], w_scaled)
            settle()
            step(v.scalar_tensor_tensor(out=hid_out, in0=w_inv[:, 1:2], scalar=2.0 ** 8, in1=w_inv[:, 1:2], op0=ALU.mult, op1=ALU.mult))
            for u in (3, 4):
                for j in range(2):
                    swiglu(0, u, j)
                w2_low(u - 3)
            dve.wait_ge(w2_lo, 2 * C2 + 2)

            with steps.loop(1, GROUPS, NORM_STEPS + TPG * (Z_STEPS + PICKS * PICK_STEPS)) as g:
                for j in range(2):
                    swiglu(g, 0, j)
                normalise(g - 1, down_ready, 1, down_out[:, bass.ds(g - 1, 1)], x1_ready)
                with steps.loop(1, U1, Z_STEPS + PICKS * PICK_STEPS) as u:
                    tile = g * TPG + u - (TPG + 1)
                    x1_low(tile)
                    swiglu(g, u, 0)
                    stack_z(tile, pick_b)
                    pick(tile, 0, pick_a)
                    swiglu(g, u, 1)
                    pick(tile, 1, pick_b)
                    pick(tile, 2, pick_a)
                    pick(tile, 3, pick_b)

            def make_mask(g, u):
                unit = g * U2 + u
                if not (isinstance(unit, int) and unit == 0):
                    dve.wait_ge(mask_t_ready, unit)
                shape = [P, TPG, 2 * BPC, SPARSITY]
                v.tensor_tensor(mask.rearrange("p (t b j) -> p t b j", t=TPG, b=2 * BPC),
                                rev16[:, :].unsqueeze(1).unsqueeze(1).broadcast_to(shape),
                                winner[:, bass.ds(g * TPG, TPG), bass.ds(u * (2 * BPC), 2 * BPC)].unsqueeze(3).broadcast_to(shape),
                                ALU.is_equal).then_inc(mask_ready, 1)

            mask_t = pick_a[:, :].bitcast(F16)

            def apply_mask(g, u):
                for j in range(2):
                    n = g * C2 + u * 2 + j
                    dve.wait_ge(relu_ready, n + 1)
                    if j == 0:
                        dve.wait_ge(mask_t_ready, g * U2 + u + 1)
                    v.tensor_tensor(act32[j], mask_t[:, j * GT:(j + 1) * GT], act32[j], ALU.mult).then_inc(masked, 1)

            settle()
            dve.wait_ge(up_ready, N1)
            make_mask(0, 0)
            apply_mask(0, 0)
            normalise(GROUPS - 1, down_ready, 1, down_out[:, GROUPS - 1:GROUPS], x1_ready)

            def units2(g, picks):
                if picks:
                    tile0 = g * 2 + (GROUPS - 1) * TPG
                    for u in range(1, U2):
                        i, part = (u - 1) // 3, (u - 1) % 3
                        make_mask(g, u)
                        if part == 0:
                            x1_low(tile0 + i)
                        else:
                            pick(tile0 + i, 2 * part - 2, pick_b)
                        apply_mask(g, u)
                        if part == 0:
                            stack_z(tile0 + i, pick_b)
                        else:
                            pick(tile0 + i, 2 * part - 1, pick_b)
                else:
                    with dve.Fori(1, U2) as u:
                        make_mask(g, u)
                        apply_mask(g, u)

            with steps.loop(0, 2, 2 * (Z_STEPS + PICKS * PICK_STEPS) + NORM_STEPS) as g:
                units2(g, True)
                make_mask(g + 1, 0)
                apply_mask(g + 1, 0)
                normalise(g, sparse_ready, 2, hid_out, rows_out)
            settle()
            units2(2, False)
            make_mask(3, 0)
            apply_mask(3, 0)
            normalise(2, sparse_ready, 2, hid_out, rows_out)
            units2(3, False)
            normalise(3, sparse_ready, 2, hid_out, rows_out)


INPUTS = ["x", "x_t", "ug_t", "point", "discount", "fuse_t", "w1_all", "c1_rep", "c2_rep", "w2_all", "consts"]


def constants():
    import numpy as np
    c = np.zeros((P, CONST_COLS), np.float32)
    for p in range(P):
        piece = p // RANK
        c[p, piece // 3] = 1
        c[p, 3 + piece % 3] = 1
    c[:, 6:6 + SPARSITY] = np.arange(SPARSITY, 0, -1)
    c[:, 6 + SPARSITY:] = np.eye(P)
    return c


def kernel(L0_attn_hidden_states, L0_attn_up_w, L0_attn_gate_w, L0_attn_local_point, L0_attn_local_approx_output,
           L0_attn_fuse_weight, L0_attn_discount_factor, L0_attn_ffn_gate_w, L0_attn_ffn_up_w, L0_attn_ffn_down_w,
           L0_ffn_c1_w, L0_ffn_c2_w, L0_ffn_w1, L0_ffn_w2t):
    import numpy as np
    import concourse.bacc as bacc
    from concourse import mybir as _mybir
    from concourse.bass_utils import run_bass_kernel_spmd

    a = np.asarray
    X = a(L0_attn_hidden_states).reshape(TOKENS, H)

    def chunks_first(w):
        return w.reshape(-1, P, KC, P).transpose(3, 0, 2, 1)

    def padded(w, axis):
        pad = [(0, 0), (0, 0)]
        pad[axis] = (0, C1 * P - F1)
        return np.pad(w, pad)

    gate, up = (chunks_first(padded(a(w), 0)).reshape(P, C1, H) for w in (L0_attn_ffn_gate_w, L0_attn_ffn_up_w))
    down = padded(a(L0_attn_ffn_down_w), 1).T.reshape(C1, P, H).transpose(1, 0, 2)
    w1 = chunks_first(a(L0_ffn_w1)).reshape(P, C2, H)
    w2 = a(L0_ffn_w2t).reshape(C2, P, H).transpose(1, 0, 2)
    fuse = np.concatenate([a(L0_attn_local_approx_output)[:, :, None], a(L0_attn_fuse_weight)], axis=2)
    ug = np.concatenate([a(L0_attn_up_w), a(L0_attn_gate_w)], axis=0)
    arrays = {
        "x": X,
        "x_t": X.T.reshape(KC, P, TOKENS).transpose(1, 0, 2),
        "ug_t": ug.T.reshape(KC, P, 2 * S).transpose(1, 0, 2).reshape(P, -1),
        "point": a(L0_attn_local_point).reshape(S, 1),
        "discount": np.tile(a(L0_attn_discount_factor).reshape(1, G), (P, 1)),
        "fuse_t": fuse.transpose(1, 2, 0).reshape(S, -1),
        "w1_all": np.stack([gate, up, down], axis=2).reshape(P, -1),
        "c1_rep": np.tile(a(L0_ffn_c1_w).T.reshape(KC, P, RANK).transpose(1, 0, 2), (1, 1, COPIES)).reshape(P, -1),
        "c2_rep": np.tile(a(L0_ffn_c2_w).T, (COPIES, 1)),
        "w2_all": np.stack([w1, w2], axis=2).reshape(P, -1),
        "consts": constants(),
    }
    arrays = {k: np.ascontiguousarray(v) for k, v in arrays.items()}
    nc = bacc.Bacc("TRN2", target_bir_lowering=False, num_devices=1)
    args = [nc.dram_tensor(f"in_{k}", arrays[k].shape, F32, kind="ExternalInput").ap() for k in INPUTS]
    args.append(nc.dram_tensor("out_0", (TOKENS, H), F32, kind="ExternalOutput").ap())
    program(nc, *args)
    r = run_bass_kernel_spmd(nc, [{f"in_{k}": v for k, v in arrays.items()}], core_ids=[0])
    return r.results[0]["out_0"].reshape(a(L0_attn_hidden_states).shape)
```

```python
from contextlib import ExitStack, contextmanager

import concourse.bass as bass
from concourse import mybir

F32 = mybir.dt.float32
F16 = mybir.dt.float16
BF16 = mybir.dt.bfloat16
I32 = mybir.dt.int32
U8 = mybir.dt.uint8
ALU = mybir.AluOpType
ACT = mybir.ActivationFunctionType
AX = mybir.AxisListType
ABSMAX = bass.bass_isa.ReduceOp.absmax

P = 128
TOKENS, H, S, G = 2048, 512, 128, 6
F1, F2, RANK, SPARSITY = 1248, 1792, 16, 32
THD, EPS = 2.5, 1e-5
KC = H // P
GT = 512
GROUPS = TOKENS // GT
TPG = GT // P
C1 = -(-F1 // P)
C2 = F2 // P
U1, U2 = C1 // 2, C2 // 2
BLOCKS = F2 // SPARSITY
COPIES = P // RANK
PICK_COLS = 448
PICKS = F2 // PICK_COLS
PB = PICK_COLS // SPARSITY
BPC = P // SPARSITY

W2_SLOT, W1_SLOT = 2 * H, 3 * H
W2_AT = 0
AUX_AT = W2_AT + C2 * W2_SLOT
AUX_WORDS = 2048
W1_AT = AUX_AT + AUX_WORDS
BIG_WORDS = W1_AT + C1 * W1_SLOT
XT_AT = W2_AT
FUSE_AT = XT_AT + 2 * KC * GT
UG_AT = FUSE_AT + (G + 1) * H
TERM_AT = UG_AT + KC * 2 * S
DELTA_AT = TERM_AT + (G + 1) * GT
assert DELTA_AT + 3 * GT <= AUX_AT

TOP = 13
X1_SCALE = 2.0 ** 9
HID_SCALE = 2.0 ** -17
CONST_COLS = 6 + SPARSITY + P

MAX_ORDER = [("x", 0), ("c1", 0), ("x", 1), ("w", 0), ("x", 2), ("w", 1), ("x", 3), ("w", 2)]
LOWER = 2.0 ** 34


class Steps:

    def __init__(self, engine, sem):
        self.engine, self.sem, self.base, self.n = engine, sem, 0, 0

    def did(self, instruction):
        instruction.then_inc(self.sem, 1)
        self.n += 1

    def settle(self):
        self.engine.wait_ge(self.sem, self.base + self.n)

    @contextmanager
    def loop(self, start, end, per):
        base, n = self.base, self.n
        with self.engine.Fori(start, end) as i:
            self.base, self.n = base + n + (i - start) * per, 0
            yield i
            assert self.n == per, (self.n, per)
        self.base, self.n = base, n + (end - start) * per


def program(nc, x, x_t, ug_t, point, discount, fuse_t, w1_all, c1_rep, c2_rep, w2_all, consts, out):
    ctx = ExitStack()
    with ctx:
        def sb(name, shape, dt):
            return ctx.enter_context(nc.sbuf_tensor(name, shape, dt))

        def sem(name):
            return ctx.enter_context(nc.semaphore(name))

        big = sb("big", [P, 2 * BIG_WORDS], F16)
        big16, big32 = big[:, :], big[:, :].bitcast(F32)
        rows = sb("rows", [P, GROUPS * TPG, H], F32)
        xs = sb("xs", [P, GROUPS * 2 * KC * GT], F16)
        work = sb("work", [P, 2 * 3072], F16)
        work32 = work[:, :].bitcast(F32)
        c2_stack = sb("c2_stack", [P, F2], BF16)
        c1_parts = sb("c1_parts", [P, 2 * KC * P], F16)
        const_sb = sb("const_sb", [P, CONST_COLS], F32)
        ident16 = sb("ident16", [P, P], F16)
        rev16 = sb("rev16", [P, SPARSITY], F16)
        winner = sb("winner", [P, GROUPS * TPG, BLOCKS], U8)
        point_sb = sb("point_sb", [P, 1], F32)
        disc_sb = sb("disc_sb", [P, G], F32)
        sc = sb("sc", [P, 64], F32)
        small = sb("small", [P, 44], F32)

        slice_mask = [const_sb[:, i:i + 1] for i in range(6)]
        ident32 = const_sb[:, 6 + SPARSITY:6 + SPARSITY + P]

        x_part, x_all = sc[:, 0:4], sc[:, 4:8]
        w_part, w_all = sc[:, 8:12], sc[:, 12:16]
        x_exp, x_scale, x_inv = sc[:, 16:20], sc[:, 20:24], sc[:, 24:28]
        w_max, w_exp, w_scale, w_inv = sc[:, 28:30], sc[:, 30:32], sc[:, 32:34], sc[:, 34:36]
        gate_out, up_out, down_out = sc[:, 36:40], sc[:, 40:44], sc[:, 44:48]
        spare, hid_out = sc[:, 48:52], sc[:, 52:53]
        factor = sc[:, 53:53 + G]
        c1_part, c1_all, c1_exp, c1_scale, c1_inv = [sc[:, i:i + 1] for i in range(59, 64)]
        stats = small[:, 0:24].rearrange("p (t s) -> p t s", t=TPG)
        mv = small[:, 24:32].rearrange("p (t s) -> p t s", t=TPG)
        ve, y, ya = small[:, 32:36], small[:, 36:40], small[:, 40:44]

        def words(at, n):
            return big32[:, at:at + n]

        xt = [words(XT_AT + i * KC * GT, KC * GT) for i in range(2)]
        fuse = [words(FUSE_AT + m * H, H) for m in range(G + 1)]
        ug = words(UG_AT, KC * 2 * S)
        term = [words(TERM_AT + m * GT, GT) for m in range(G + 1)]
        delta, keep, delta_keep = [words(DELTA_AT + i * GT, GT) for i in range(3)]

        w1_raw = words(W1_AT - W1_SLOT, C1 * W1_SLOT)
        w2_raw = words(W2_AT + W2_SLOT, C2 * W2_SLOT)

        def w1_part(s, k, part):
            at = 2 * W1_AT + k * 2 * H + part * H
            return lambda a, n: big16[:, bass.ds(s * (2 * W1_SLOT) + (at + a), n)]

        def w2_part(c, k, part):
            at = 2 * W2_AT + k * 2 * H + part * H
            return lambda a, n: big16[:, bass.ds(c * (2 * W2_SLOT) + (at + a), n)]

        def x_part16(g, part, kc, a=0, n=GT):
            return xs[:, bass.ds(g * (2 * KC * GT) + ((part * KC + kc) * GT + a), n)]

        act32 = [work32[:, j * GT:(j + 1) * GT] for j in range(2)]

        def act_part(pair, j, part, a=0, n=GT):
            return work[:, bass.ds((pair % 2) * (4 * GT) + (4 * GT + (2 * j + part) * GT + a), n)]

        c2_raw = work32[:, 0:F2]
        c2_round = work[:, 2 * F2:3 * F2].bitcast(BF16)
        assert 3 * F2 <= 6144
        c1_raw = xs[:, (GROUPS - 1) * 2 * KC * GT:(GROUPS - 1) * 2 * KC * GT + 2 * KC * P].bitcast(F32)

        a32 = AUX_AT
        x1_part = [big16[:, 2 * a32 + i * H:2 * a32 + (i + 1) * H] for i in range(2)]
        a16 = 2 * (a32 + H)
        z_rest = words(a32 + H, P)
        z_hi = big16[:, a16 + 256:a16 + 384].bitcast(BF16)
        z_mid = big16[:, a16 + 384:a16 + 512].bitcast(BF16)
        z_stack = big16[:, a16 + 512:a16 + 640].bitcast(BF16)
        hit = [big16[:, a16 + 640 + i * PICK_COLS:a16 + 640 + (i + 1) * PICK_COLS] for i in range(2)]
        rank = [big16[:, a16 + 1536 + i * PICK_COLS:a16 + 1536 + (i + 1) * PICK_COLS] for i in range(2)]
        block_max = [words(a32 + H + 1216 + i * 16, PB) for i in range(2)]
        lower16 = words(a32 + H + 1248, P // 2).bitcast(BF16)
        assert a32 + H + 1248 + P // 2 <= W1_AT
        mask_at = 2 * (W1_AT + 5 * W1_SLOT)
        mask = big16[:, mask_at:mask_at + TPG * 2 * P].bitcast(BF16)

        def bank(name):
            return ctx.enter_context(nc.psum_tensor(name, [P, 512], F32))

        pa, pb, pick_a, pick_b = bank("pa"), bank("pb"), bank("pick_a"), bank("pick_b")
        acc = [bank(f"acc{t}") for t in range(TPG)]
        pick_bank = [pick_a, pick_b]

        fuse_in = [sem(f"fuse_in{i}") for i in range(3)]
        vectors_in, small_in, c2_in = sem("vectors_in"), sem("small_in"), sem("c2_in")
        first_in = [sem(f"first_in{kc}") for kc in range(KC)]
        xt_in = [sem("xt_in0"), sem("xt_in1")]
        rows_in = [sem(f"rows_in{g}") for g in range(GROUPS)]
        w1_in = [sem("w1_in0"), sem("w1_in1")]
        w2_in = [sem("w2_in0"), sem("w2_in1")]
        out_done = sem("out_done")
        u_ready, delta_pre_ready, taylor_ready = sem("u_ready"), sem("delta_pre_ready"), sem("taylor_ready")
        gate_ready, up_ready, down_ready = sem("gate_ready"), sem("up_ready"), sem("down_ready")
        x1t_ready, z_ready, score_ready = sem("x1t_ready"), sem("z_ready"), sem("score_ready")
        hid_ready, sparse_ready = sem("hid_ready"), sem("sparse_ready")
        factor_ready, fuse_scaled, u_copied, xhi_ready = sem("factor_ready"), sem("fuse_scaled"), sem("u_copied"), sem("xhi_ready")
        silu_ready, act_hi = sem("silu_ready"), sem("act_hi")
        w1_hi, w2_hi = sem("w1_hi"), sem("w2_hi")
        x1_hi, x1t_copied, c1_hi = sem("x1_hi"), sem("x1t_copied"), sem("c1_hi")
        act_lo, max_ready = sem("act_lo"), sem("max_ready")
        vstep = sem("vstep")
        delta_ready, terms_ready, banks_added = sem("delta_ready"), sem("terms_ready"), sem("banks_added")
        max_part, x_scaled, w_scaled, xlo_ready = sem("max_part"), sem("x_scaled"), sem("w_scaled"), sem("xlo_ready")
        w1_lo, w2_lo, swiglu_ready = sem("w1_lo"), sem("w2_lo"), sem("swiglu_ready")
        x1_ready, x1_lo, z_stacked, score_used = sem("x1_ready"), sem("x1_lo"), sem("z_stacked"), sem("score_used")
        c1_scaled, c1_lo = sem("c1_scaled"), sem("c1_lo")
        c2_stacked, mask_ready, rows_out = sem("c2_stacked"), sem("mask_ready"), sem("rows_out")

        W2_UNIT, W2_FIRST = 5, 2
        W1_EARLY = 3
        N1 = GROUPS * C1
        def added(phase, g, t):
            return TPG * (1 + GROUPS * phase) + TPG * g + (t + 1)

        act_passed, vector_passed, tensor_passed = sem("act_passed"), sem("vector_passed"), sem("tensor_passed")

        def apart(engine, passed):
            engine.sem_inc(passed, 1)

        block = ctx.enter_context(nc.Block())

        @block.sync
        def _(sp):
            for kc in range(KC):
                sp.dma_start(ug[:, kc * 2 * S:(kc + 1) * 2 * S], ug_t[:, kc * 2 * S:(kc + 1) * 2 * S]).then_inc(first_in[kc], 16)
                sp.dma_start(xt[0][:, kc * GT:(kc + 1) * GT], x_t[:, kc, 0:GT]).then_inc(first_in[kc], 16)

            def load_xt(g):
                sp.dma_start(xt[g % 2].rearrange("p (k t) -> p k t", k=KC),
                             x_t[:, :, g * GT:(g + 1) * GT]).then_inc(xt_in[g % 2], 16)

            def load_rows(g):
                sp.dma_start(rows[:, g * TPG:(g + 1) * TPG, :],
                             x[g * GT:(g + 1) * GT, :].rearrange("(t p) m -> p t m", p=P)).then_inc(rows_in[g], 16)

            for dst, src in ((point_sb[:, :], point), (disc_sb[:, :], discount)):
                sp.dma_start(dst, src).then_inc(vectors_in, 16)
            for i, (m0, m1) in enumerate(((0, 1), (1, 4), (4, G + 1))):
                sp.dma_start(words(FUSE_AT + m0 * H, (m1 - m0) * H), fuse_t[:, m0 * H:m1 * H]).then_inc(fuse_in[i], 16)
            for dst, src in ((const_sb[:, :], consts), (c1_raw, c1_rep)):
                sp.dma_start(dst, src).then_inc(small_in, 16)
            load_xt(1)
            load_rows(0)
            sp.dma_start(c2_raw, c2_rep).then_inc(c2_in, 16)
            half = C1 // 2 * W1_SLOT
            for i in range(2):
                sp.dma_start(w1_raw[:, i * half:(i + 1) * half], w1_all[:, i * half:(i + 1) * half]).then_inc(w1_in[i], 16)
                load_rows(1 + i)
                g = 2 + i
                sp.wait_ge(delta_pre_ready, g - 1)
                sp.wait_ge(xlo_ready, g - 1)
                load_xt(g)
            load_rows(3)
            sp.wait_ge(taylor_ready, GROUPS * TPG)
            sp.wait_ge(xlo_ready, GROUPS)
            sp.wait_ge(w1_lo, 3 * C1)
            half = C2 // 2 * W2_SLOT
            for i in range(2):
                sp.dma_start(w2_raw[:, i * half:(i + 1) * half], w2_all[:, i * half:(i + 1) * half]).then_inc(w2_in[i], 16)
            for g in range(GROUPS - 1):
                sp.wait_ge(rows_out, TPG * (g + 1))
                sp.dma_start(out[g * GT:(g + 1) * GT, :].rearrange("(t p) m -> p t m", p=P),
                             rows[:, g * TPG:(g + 1) * TPG, :]).then_inc(out_done, 16)
            for t in range(TPG):
                tile = (GROUPS - 1) * TPG + t
                sp.wait_ge(rows_out, tile + 1)
                sp.dma_start(out[tile * P:(tile + 1) * P, :], rows[:, tile, :]).then_inc(out_done, 16)
            sp.wait_ge(out_done, 16 * (GROUPS - 1 + TPG))

        @block.tensor
        def _(pe):
            def split_product(dst, weights, g, stop=True):
                apart(pe, tensor_passed)
                for kc in range(KC):
                    for wp, xp in ((0, 0), (0, 1), (1, 0)):
                        mm = nc.tensor.matmul(dst[:, :], weights(wp)(kc * P, P), x_part16(g, xp, kc),
                                              start=(kc == 0 and wp == xp), stop=(stop and kc == KC - 1 and wp == 1))
                return mm

            def second_product(pair, j, weights, first, last, done=None, free=None):
                for t in range(TPG):
                    if free is not None:
                        pe.wait_ge(banks_added, free(t))
                    if t == 0 or free is not None:
                        apart(pe, tensor_passed)
                    for ap, wp in ((0, 0), (0, 1), (1, 0)):
                        mm = nc.tensor.matmul(acc[t][:, :], act_part(pair, j, ap, t * P, P), weights(wp)(0, H),
                                              start=(first and ap == wp), stop=(last and ap == 1))
                    if done is not None:
                        mm.then_inc(done, 1)

            ug_v = ug.rearrange("p (k s) -> p k s", k=KC)
            def phase0(g, i):
                for dst, col, done in ((pa, 0, u_ready), (pb, S, delta_pre_ready)):
                    for kc in range(KC):
                        if g == 0 and col == 0:
                            pe.wait_ge(first_in[kc], 32)
                        mm = nc.tensor.matmul(dst[:, :], ug_v[:, kc, col:col + S], xt[i][:, kc * GT:(kc + 1) * GT],
                                              start=(kc == 0), stop=(kc == KC - 1))
                    mm.then_inc(done, 1)
                for m in range(G + 1):
                    if m == 0:
                        pe.wait_ge(u_copied, g + 1)
                        pe.wait_ge(fuse_in[0], 16)
                        pe.wait_ge(banks_added, g * TPG + TPG)
                    else:
                        pe.wait_ge(terms_ready, g * G + m)
                        pe.wait_ge(fuse_scaled, m)
                    for t in range(TPG):
                        mm = nc.tensor.matmul(acc[t][:, :], term[m][:, t * P:(t + 1) * P], fuse[m],
                                              start=(m == 0), stop=(m == G))
                        if m == G:
                            mm.then_inc(taylor_ready, 1)

            for g in range(GROUPS):
                if g:
                    pe.wait_ge(xt_in[g % 2], (g + 1) // 2 * 16)
                phase0(g, g % 2)

            def transposes(tile, dst, free):
                pe.wait_ge(x1_lo, tile + 1)
                pe.wait_ge(score_used, free)
                for part in range(2):
                    for kc in range(KC):
                        mm = nc.tensor.transpose(dst[:, :].bitcast(F16)[:, part * H + kc * P:part * H + (kc + 1) * P],
                                                 x1_part[part][:, kc * P:(kc + 1) * P], ident16[:, :])
                mm.then_inc(x1t_ready, 1)

            def z_product(tile, g, t, dst, free):
                pe.wait_ge(score_used, free)
                pe.wait_ge(x1t_copied, tile + 1)
                for kc in range(KC):
                    for wp, xp in ((0, 0), (0, 1), (1, 0)):
                        mm = nc.tensor.matmul(dst[:, 0:P], c1_parts[:, (wp * KC + kc) * P:(wp * KC + kc + 1) * P],
                                              x_part16(g, xp, kc, t * P, P),
                                              start=(kc == 0 and wp == xp), stop=(kc == KC - 1 and wp == 1))
                mm.then_inc(z_ready, 1)

            def scores(tile, k, dst):
                pe.wait_ge(z_stacked, tile + 1)
                nc.tensor.matmul(dst[:, 0:PICK_COLS], z_stack, c2_stack[:, k * PICK_COLS:(k + 1) * PICK_COLS],
                                 start=True, stop=True).then_inc(score_ready, 1)

            def unit1(g, u, tile=None, start=False):
                for j in range(2):
                    n = g * C1 + u * 2 + j
                    s = (C1 - 1 - j) - u * 2
                    if not (start and j == 0):
                        pe.wait_ge(silu_ready, n)
                    split_product(pa, lambda part: w1_part(s, 0, part), g).then_inc(gate_ready, 1)
                    if tile is not None:
                        if j == 1:
                            pe.wait_ge(score_used, tile * PICKS + (PICKS + 1))
                        scores(tile, 2 * j, pick_a)
                    if not (start and j == 0):
                        pe.wait_ge(swiglu_ready, n)
                    split_product(pb, lambda part: w1_part(s, 1, part), g).then_inc(up_ready, 1)
                    if tile is not None:
                        if j == 1:
                            pe.wait_ge(score_used, tile * PICKS + (PICKS + 2))
                        scores(tile, 2 * j + 1, pick_b)

            def down(g, u, kind, tile=None):
                before = g * U1 + u - 1
                for j in range(2):
                    m = before * 2 + j
                    slot = (C1 - 1 - j) - (u - 1) * 2 if kind != "last" else 1 - j
                    pe.wait_ge(act_lo, m + 1)
                    first, last = kind == "first" and j == 0, kind == "last" and j == 1
                    second_product(before, j, lambda part: w1_part(slot, 2, part), first, last,
                                   done=down_ready if last else None,
                                   free=(lambda t: added(1, g - 1, t)) if first else None)
                    if tile is not None:
                        if j == 0:
                            transposes(tile, pick_a, tile * PICKS + 3)
                        else:
                            z_product(tile, g - 1, u - 1, pick_b, tile * PICKS + 4)

            pe.wait_ge(xlo_ready, GROUPS)
            pe.wait_ge(c1_lo, 1)
            pe.wait_ge(c2_stacked, 1)
            pe.wait_ge(banks_added, added(0, GROUPS - 1, TPG - 1))
            pe.wait_ge(w1_lo, 3 * 2)
            pe.wait_ge(u_copied, GROUPS)
            pe.wait_ge(delta_ready, GROUPS)
            unit1(0, 0, start=True)
            pe.wait_ge(w1_lo, 3 * C1)
            def group1(g, picks):
                t = (lambda u: (g - 1) * TPG + (u - 1)) if picks else (lambda u: None)
                unit1(g, 1)
                down(g, 1, "first", t(1))
                with pe.Fori(2, U1) as u:
                    unit1(g, u, t(u - 1))
                    down(g, u, "middle", t(u))

            group1(0, False)
            unit1(1, 0)
            down(1, 0, "last")
            with pe.Fori(1, GROUPS - 1) as g:
                group1(g, True)
                unit1(g + 1, 0, g * TPG - 1)
                down(g + 1, 0, "last")
            group1(GROUPS - 1, True)

            def second2(g, u, kind, after_first):
                before = g * U2 + u - 1
                for j in range(2):
                    c = (u - 1) * 2 + j if kind != "last" else C2 - 2 + j
                    pe.wait_ge(act_lo, N1 + before * 2 + j + 1)
                    first, last = kind == "first" and j == 0, kind == "last" and j == 1
                    second_product(before + GROUPS * U1, j, lambda part: w2_part(c, 1, part), first, last,
                                   done=sparse_ready if last else None,
                                   free=(lambda t: added(2, g - 1, t)) if first else None)
                    if j == 0:
                        after_first()

            def hidden(dst, c, g, unit, j):
                apart(pe, tensor_passed)
                split_product(dst, lambda part: w2_part(c, 0, part), g, stop=False)
                if j == 0:
                    pe.wait_ge(mask_ready, unit + 1)
                for t in range(TPG):
                    mm = nc.tensor.matmul(dst[:, t * P:(t + 1) * P], mask[:, (t * 2 + j) * P:(t * 2 + j + 1) * P],
                                          lower16, start=False, stop=(t == TPG - 1))
                mm.then_inc(hid_ready, 1)

            def unit2(g, u, after_first, after_hidden, after_third, kind, start=False, by_tile=False):
                for j, dst in enumerate((pa, pb)):
                    n = g * C2 + u * 2 + j
                    if not start:
                        pe.wait_ge(act_hi, N1 + n - 1)
                    hidden(dst, u * 2 + j, g, g * U2 + u, j)
                    (after_first, after_hidden)[j]()
                if kind == "phase 1":
                    before = GROUPS * U1 - 1
                    for j in range(2):
                        pe.wait_ge(act_lo, before * 2 + j + 1)
                        second_product(before, j, lambda part: w1_part(1 - j, 2, part), False, j == 1,
                                       done=down_ready if j else None)
                        if j == 0:
                            after_third()
                    return
                second2(g, u, kind, after_third)

            pe.wait_ge(w2_lo, 2 * C2 + 2)
            pe.wait_ge(silu_ready, N1)
            pe.wait_ge(swiglu_ready, N1)
            def none():
                pass

            def s(tile, k):
                def go():
                    if k >= 2:
                        pe.wait_ge(score_used, tile * PICKS + (PICKS + k - 1))
                    scores(tile, k, pick_bank[k % 2])
                return go

            tile = (GROUPS - 1) * TPG - 1

            def first_two():
                s(tile, 0)()
                s(tile, 1)()

            unit2(0, 0, first_two, s(tile, 2), s(tile, 3), "phase 1", start=True)

            def z2(tile):
                return lambda: z_product(tile, GROUPS - 1, tile - (GROUPS - 1) * TPG, pick_b, tile * PICKS + 4)

            with pe.Fori(0, 2) as g:
                for i in range(2):
                    tile = g * 2 + ((GROUPS - 1) * TPG + i)
                    if i == 0:
                        unit2(g, 1, none, none, none, "first")
                        transposes(tile, pick_a, tile * PICKS + 3)
                    unit2(g, 3 * i + 2, z2(tile), none, s(tile, 0), "middle")
                    unit2(g, 3 * i + 3, s(tile, 1), none, s(tile, 2), "middle")
                    if i == 0:
                        unit2(g, 4, s(tile, 3), none, none, "middle")
                        transposes(tile + 1, pick_a, tile * PICKS + (PICKS + 3))
                    else:
                        unit2(g + 1, 0, s(tile, 3), none, none, "last")
            for g in (2, 3):
                unit2(g, 1, none, none, none, "first")
                with pe.Fori(2, U2) as u:
                    unit2(g, u, none, none, none, "middle")
                if g == 2:
                    unit2(3, 0, none, none, none, "last")
            before = GROUPS * U2 - 1
            pe.wait_ge(act_lo, N1 + before * 2 + 2)
            for t in range(TPG):
                for j in range(2):
                    for ap, wp in ((0, 0), (0, 1), (1, 0)):
                        mm = nc.tensor.matmul(acc[t][:, :], act_part(before + GROUPS * U1, j, ap, t * P, P),
                                              w2_part(C2 - 2 + j, 1, wp)(0, H), start=False, stop=(j == 1 and ap == 1))
                mm.then_inc(sparse_ready, 1)

        @block.scalar
        def _(act):
            act.wait_ge(vectors_in, 16 * 2)
            def copy_u(g):
                act.wait_ge(u_ready, g + 1)
                act.activation(term[0], pa[:, :], ACT.Copy).then_inc(u_copied, 1)

            act.activation(factor, disc_sb[:, :], ACT.Exp, scale=-1.0).then_inc(factor_ready, 1)
            act.wait_ge(factor_ready, 1)
            for m in range(1, G + 1):
                act.wait_ge(fuse_in[1 + (m > 3)], 16)
                if m == 3:
                    copy_u(0)
                act.activation(fuse[m], fuse[m], ACT.Copy, scale=factor[:, m - 1:m]).then_inc(fuse_scaled, 1)

            def x_hi(g, i):
                act.wait_ge(x_scaled, g + 1)
                act.activation(xs[:, bass.ds(g * (2 * KC * GT), KC * GT)], xt[i], ACT.Copy,
                               scale=x_scale[:, bass.ds(g, 1)]).then_inc(xhi_ready, 1)

            def w1_high(d0, d1):
                for d in range(d0, d1):
                    s = C1 - 1 - d
                    for k in range(3):
                        if d:
                            act.wait_ge(w1_lo, 3 * (d - 1) + k + 1)
                        act.activation(w1_part(s, k, 0)(0, H), w1_raw[:, s * W1_SLOT + k * H:s * W1_SLOT + (k + 1) * H],
                                       ACT.Copy, scale=w_scale[:, 0:1]).then_inc(w1_hi, 1)

            for g in range(GROUPS):
                if g:
                    copy_u(g)
                x_hi(g, g % 2)
                if g == 0:
                    act.wait_ge(c1_scaled, 1)
                    act.activation(c1_parts[:, 0:KC * P], c1_raw, ACT.Copy, scale=c1_scale).then_inc(c1_hi, 1)
                if g == 2:
                    act.wait_ge(w_scaled, 1)
                    w1_high(0, W1_EARLY)
            w1_high(W1_EARLY, C1)


            def swiglu(g, u, start=False, tile=None, weights=None):
                pair = g * U1 + u
                for j in range(2):
                    n = g * C1 + u * 2 + j
                    act.wait_ge(gate_ready, n + 1)
                    if not start:
                        act.wait_ge(act_lo, n - 1)
                    apart(act, act_passed)
                    act.activation(act32[j], pa[:, :], ACT.Silu, scale=gate_out[:, bass.ds(g, 1)]).then_inc(silu_ready, 1)
                    if weights is not None and j == 1:
                        w2_high(weights + 1, weights + 2)
                    act.wait_ge(swiglu_ready, n + 1)
                    apart(act, act_passed)
                    act.activation(act_part(pair, j, 0), act32[j], ACT.Copy).then_inc(act_hi, 1)
                    if weights is not None and j == 0:
                        w2_high(weights, weights + 1)
                    if tile is not None:
                        if j == 0:
                            x1_high(tile)
                        else:
                            x1t_copy(g - 1, u - 1, pick_a)
                if weights is not None:
                    w2_high(weights + W2_FIRST, min(weights + W2_UNIT, C2))

            def x1_high(tile):
                act.wait_ge(x1_ready, tile + 1)
                apart(act, act_passed)
                act.activation(x1_part[0], rows[:, bass.ds(tile, 1), :].rearrange("p a m -> p (a m)"), ACT.Copy,
                               scale=X1_SCALE).then_inc(x1_hi, 1)

            def x1t_copy(g, t, src):
                act.wait_ge(x1t_ready, g * TPG + (t + 1))
                apart(act, act_passed)
                dst = xs[:, bass.ds(g * (2 * KC * GT), 2 * KC * GT)].rearrange("p (k t) -> p k t", k=2 * KC)
                act.activation(dst[:, :, bass.ds(t * P, P)], src[:, :].bitcast(F16).rearrange("p (k t) -> p k t", k=2 * KC),
                               ACT.Copy).then_inc(x1t_copied, 1)

            def w2_high(c0, c1):
                act.wait_ge(w_scaled, 2)
                with act.Fori(c0, c1) as c:
                    for k in range(2):
                        act.wait_ge(w2_lo, c * 2 + (k + 1))
                        apart(act, act_passed)
                        act.activation(w2_part(c, k, 0)(0, H), big32[:, bass.ds(c * W2_SLOT + (W2_AT + W2_SLOT + k * H), H)],
                                       ACT.Copy, scale=w_scale[:, 1:2]).then_inc(w2_hi, 1)

            swiglu(0, 0, start=True)
            with act.Fori(1, 3) as u:
                swiglu(0, u)
            for i in range(3):
                swiglu((3 + i) // U1, (3 + i) % U1, weights=i * W2_UNIT)
            act.wait_ge(w2_lo, 2 * C2 + 2)
            with act.Fori(1, GROUPS - 1) as g:
                with act.Fori(1, U1) as u:
                    swiglu(g, u, tile=g * TPG + u - (TPG + 1))
                swiglu(g + 1, 0)
            with act.Fori(1, U1) as u:
                swiglu(GROUPS - 1, u, tile=u + (GROUPS - 1) * TPG - (TPG + 1))

            def hidden(g, u, t=None):
                for j in range(2):
                    n = g * C2 + u * 2 + j
                    act.wait_ge(hid_ready, n + 1)
                    act.wait_ge(act_lo, N1 + n - 1)
                    apart(act, act_passed)
                    act.activation(act32[j], (pa, pb)[j][:, :], ACT.Relu, scale=HID_SCALE)
                    act.activation(act_part(GROUPS * U1 + g * U2 + u, j, 0), (pa, pb)[j][:, :], ACT.Relu,
                                   scale=HID_SCALE).then_inc(act_hi, 1)
                if t is not None:
                    x1_high(t + (GROUPS - 1) * TPG)
                    x1t_copy(GROUPS - 1, t, pick_a)

            with act.Fori(0, 2) as g:
                hidden(g, 0)
                for i in range(2):
                    hidden(g, 3 * i + 1, g * 2 + i)
                    hidden(g, 3 * i + 2)
                    hidden(g, 3 * i + 3)
            with act.Fori(2, GROUPS) as g:
                with act.Fori(0, U2) as u:
                    hidden(g, u)

        @block.gpsimd
        def _(pool):
            def reduce_max(i):
                what, col = MAX_ORDER[i]
                part, whole = {"x": (x_part, x_all), "w": (w_part, w_all), "c1": (c1_part, c1_all)}[what]
                pool.wait_ge(max_part, i + 1)
                nc.gpsimd.partition_all_reduce(whole[:, col:col + 1], part[:, col:col + 1], P, ABSMAX).then_inc(max_ready, 1)

            def low(pair, j, n):
                pool.wait_ge(act_hi, n + 1)
                nc.gpsimd.tensor_tensor(act_part(pair, j, 1), act32[j], act_part(pair, j, 0), ALU.subtract).then_inc(act_lo, 1)

            for i in range(7):
                reduce_max(i)
            with pool.Fori(0, 3) as u:
                for j in range(2):
                    low(u, j, u * 2 + j)
            reduce_max(7)
            with pool.Fori(3, GROUPS * (U1 + U2)) as u:
                for j in range(2):
                    low(u, j, u * 2 + j)

        @block.vector
        def _(dve):
            v = nc.vector
            steps = Steps(dve, vstep)
            step, settle = steps.did, steps.settle
            dve.sem_inc(banks_added, TPG)
            dve.sem_inc(score_used, PICKS)
            dve.sem_inc(w2_lo, 2)

            def power_scales(m, e, s, inv, signal):
                m, e, s, inv = (a.bitcast(I32) for a in (m, e, s, inv))
                step(v.tensor_scalar(e, m, 0x7F800000, None, ALU.bitwise_and))
                settle()
                step(v.tensor_scalar(e, e, float((127 - 40) << 23), float((127 + 40) << 23), ALU.max, ALU.min))
                settle()
                step(v.tensor_scalar(inv, e, float(-(TOP << 23)), None, ALU.add))
                v.tensor_scalar(s, e, -1.0, float((254 + TOP) << 23), ALU.mult, ALU.add).then_inc(signal, 1)

            def take_tile(tile, t, scalar):
                r = rows[:, bass.ds(tile, 1), :].rearrange("p a m -> p (a m)")
                v.scalar_tensor_tensor(out=r, in0=acc[t][:, :], scalar=scalar, in1=r,
                                       op0=ALU.mult, op1=ALU.add).then_inc(banks_added, 1)

            def small_constants():
                dve.wait_ge(small_in, 16 * 2)
                step(v.tensor_copy(ident16[:, :], ident32))
                step(v.tensor_copy(rev16[:, :], const_sb[:, 6:6 + SPARSITY]))

            def stack_c2():
                dve.wait_ge(c2_in, 16)
                for i in range(3):
                    step(v.tensor_copy(c2_round, c2_raw))
                    settle()
                    if i == 0:
                        step(v.tensor_scalar(c2_stack[:, :], c2_round, slice_mask[3], None, ALU.mult))
                    else:
                        ins = v.scalar_tensor_tensor(out=c2_stack[:, :], in0=c2_round, scalar=slice_mask[3 + i],
                                                     in1=c2_stack[:, :], op0=ALU.mult, op1=ALU.add)
                        step(ins) if i == 1 else ins.then_inc(c2_stacked, 1)
                    if i < 2:
                        step(v.tensor_tensor(c2_raw, c2_raw, c2_round, ALU.subtract))
                        settle()
                dve.wait_ge(c2_stacked, 1)

            def weights_max(i, src, halves, col):
                dve.wait_ge(halves[i], 16)
                half = src.shape[1] // 2
                v.tensor_reduce(w_part[:, col:col + 1], src[:, i * half:(i + 1) * half], axis=AX.X, op=ALU.max,
                                apply_absolute_value=True).then_inc(max_part, 1)

            def w1_low(d0, d1):
                for d in range(d0, d1):
                    s = C1 - 1 - d
                    for k in range(3):
                        dve.wait_ge(w1_hi, 3 * d + k + 1)
                        v.scalar_tensor_tensor(out=w1_part(s, k, 1)(0, H), in0=w1_raw[:, s * W1_SLOT + k * H:s * W1_SLOT + (k + 1) * H],
                                               scalar=w_scale[:, 0:1], in1=w1_part(s, k, 0)(0, H),
                                               op0=ALU.mult, op1=ALU.subtract).then_inc(w1_lo, 1)

            def scale_phase1():
                dve.wait_ge(max_ready, MAX_ORDER.index(("w", 1)) + 1)
                step(v.tensor_tensor(w_max[:, 0:1], w_all[:, 0:1], w_all[:, 1:2], ALU.max))
                settle()
                power_scales(w_max[:, 0:1], w_exp[:, 0:1], w_scale[:, 0:1], w_inv[:, 0:1], w_scaled)

            def scale_phase1_sums():
                dve.wait_ge(w_scaled, 1)
                dve.wait_ge(x_scaled, GROUPS)
                settle()
                step(v.tensor_scalar(gate_out, x_inv, w_inv[:, 0:1], None, ALU.mult))
                step(v.tensor_scalar(up_out, x_scale, w_scale[:, 0:1], 2.0 ** -59, ALU.mult, ALU.mult))
                settle()
                step(v.scalar_tensor_tensor(out=spare, in0=gate_out, scalar=2.0 ** 59, in1=gate_out, op0=ALU.mult, op1=ALU.mult))
                settle()
                step(v.tensor_scalar(down_out, spare, w_inv[:, 0:1], None, ALU.mult))
                settle()

            for g in range(GROUPS):
                i = g % 2
                if g == 0:
                    for kc in range(KC):
                        dve.wait_ge(first_in[kc], 32)
                else:
                    dve.wait_ge(xt_in[i], 16 * ((g + 1) // 2))
                v.tensor_reduce(x_part[:, g:g + 1], xt[i], axis=AX.X, op=ALU.max,
                                apply_absolute_value=True).then_inc(max_part, 1)
                dve.wait_ge(vectors_in, 16 * 2)
                dve.wait_ge(delta_pre_ready, g + 1)
                v.tensor_scalar(delta, pb[:, :], point_sb[:, 0:1], None, ALU.subtract).then_inc(delta_ready, 1)
                dve.wait_ge(delta_ready, g + 1)
                dve.wait_ge(u_copied, g + 1)
                v.tensor_tensor(term[1], term[0], delta, ALU.mult).then_inc(terms_ready, 1)
                step(v.scalar_tensor_tensor(out=keep, in0=delta, scalar=-THD, in1=delta, op0=ALU.is_ge, op1=ALU.mult))
                settle()
                step(v.scalar_tensor_tensor(out=delta_keep, in0=delta, scalar=THD, in1=keep, op0=ALU.is_le, op1=ALU.mult))
                for m in range(2, G + 1):
                    dve.wait_ge(terms_ready, g * G + m - 1)
                    if m == 5:
                        settle()
                    v.tensor_tensor(term[m], term[m - 1], delta_keep if m == 5 else delta, ALU.mult).then_inc(terms_ready, 1)
                    if m == 3:
                        dve.wait_ge(max_ready, MAX_ORDER.index(("x", g)) + 1)
                        power_scales(x_all[:, g:g + 1], x_exp[:, g:g + 1], x_scale[:, g:g + 1], x_inv[:, g:g + 1], x_scaled)
                dve.wait_ge(xhi_ready, g + 1)
                lo = xs[:, ((g * 2 + 1) * KC) * GT:((g * 2 + 2) * KC) * GT]
                hi = xs[:, (g * 2 * KC) * GT:((g * 2 + 1) * KC) * GT]
                v.scalar_tensor_tensor(out=lo, in0=xt[i], scalar=x_scale[:, g:g + 1], in1=hi,
                                       op0=ALU.mult, op1=ALU.subtract).then_inc(xlo_ready, 1)
                if g == 0:
                    small_constants()
                    v.tensor_reduce(c1_part, c1_raw, axis=AX.X, op=ALU.max, apply_absolute_value=True).then_inc(max_part, 1)
                    dve.wait_ge(max_ready, 2)
                    power_scales(c1_all, c1_exp, c1_scale, c1_inv, c1_scaled)
                    dve.wait_ge(c1_hi, 1)
                    v.scalar_tensor_tensor(out=c1_parts[:, KC * P:2 * KC * P], in0=c1_raw, scalar=c1_scale,
                                           in1=c1_parts[:, 0:KC * P], op0=ALU.mult, op1=ALU.subtract).then_inc(c1_lo, 1)
                if g == 1:
                    stack_c2()
                    weights_max(0, w1_raw, w1_in, 0)
                if g == 2:
                    weights_max(1, w1_raw, w1_in, 1)
                    scale_phase1()
                    w1_low(0, W1_EARLY)
                if g == 3:
                    scale_phase1_sums()
                    w1_low(W1_EARLY, C1 - 1)
                dve.wait_ge(rows_in[g], 16)
                for t in range(TPG):
                    dve.wait_ge(taylor_ready, g * TPG + t + 1)
                    take_tile(g * TPG + t, t, 1.0)

            w1_low(C1 - 1, C1)

            dve.wait_ge(w1_lo, 3 * C1)
            step(v.tensor_scalar(lower16, ident32, -LOWER, None, ALU.mult))

            def swiglu(g, u, j):
                n = g * C1 + u * 2 + j
                dve.wait_ge(up_ready, n + 1)
                dve.wait_ge(silu_ready, n + 1)
                v.scalar_tensor_tensor(out=act32[j], in0=pb[:, :], scalar=up_out[:, bass.ds(g, 1)], in1=act32[j],
                                       op0=ALU.mult, op1=ALU.mult).then_inc(swiglu_ready, 1)

            def row(g, t):
                return rows[:, bass.ds(g * TPG + t, 1), :].rearrange("p a m -> p (a m)")

            def take(g, ready, scalar, tiles=range(TPG)):
                for t in tiles:
                    dve.wait_ge(ready, g * TPG + (t + 1))
                    take_tile(g * TPG + t, t, scalar)

            def moments(g, phase, tiles=range(TPG)):
                for t in tiles:
                    dve.wait_ge(banks_added, added(phase, g, t))
                    apart(dve, vector_passed)
                    step(v.bn_stats(stats[:, t, :], row(g, t)))
                settle()
                apart(dve, vector_passed)
                for t in tiles:
                    step(v.bn_aggr(mv[:, t, :], stats[:, t, :]))

            def normalise(g, signal, tiles=range(TPG)):
                at = slice(tiles[0], tiles[-1] + 1)
                ve_, y_, ya_ = ve[:, at], y[:, at], ya[:, at]
                settle()
                step(v.tensor_scalar(ve_, mv[:, at, 1], EPS, None, ALU.add))
                settle()
                step(v.tensor_scalar(ya_.bitcast(I32), ve_.bitcast(I32), 1, None, ALU.logical_shift_right))
                settle()
                step(v.tensor_scalar(y_.bitcast(I32), ya_.bitcast(I32), -1.0, float(0x5F3759DF), ALU.mult, ALU.add))
                settle()
                for _ in range(NEWTON):
                    step(v.scalar_tensor_tensor(out=ya_, in0=y_, scalar=-0.5, in1=y_, op0=ALU.mult, op1=ALU.mult))
                    settle()
                    step(v.tensor_tensor(ya_, ya_, ve_, ALU.mult))
                    settle()
                    step(v.scalar_tensor_tensor(out=y_, in0=ya_, scalar=1.5, in1=y_, op0=ALU.add, op1=ALU.mult))
                    settle()
                for t in tiles:
                    v.tensor_scalar(row(g, t), row(g, t), mv[:, t, 0:1], y[:, t:t + 1],
                                    ALU.subtract, ALU.mult).then_inc(signal, 1)

            NEWTON = 3
            NORM_STEPS = 2 * TPG + 3 + 3 * NEWTON

            def x1_low(tile):
                dve.wait_ge(x1_hi, tile + 1)
                v.scalar_tensor_tensor(out=x1_part[1], in0=rows[:, bass.ds(tile, 1), :].rearrange("p a m -> p (a m)"),
                                       scalar=X1_SCALE, in1=x1_part[0], op0=ALU.mult, op1=ALU.subtract).then_inc(x1_lo, 1)

            def stack_z(tile, src):
                dve.wait_ge(z_ready, tile + 1)
                z = src[:, 0:P]
                step(v.tensor_copy(z_hi, z))
                settle()
                step(v.tensor_tensor(z_rest, z, z_hi, ALU.subtract))
                settle()
                step(v.tensor_copy(z_mid, z_rest))
                settle()
                step(v.tensor_tensor(z_rest, z_rest, z_mid, ALU.subtract))
                settle()
                step(v.tensor_scalar(z_stack, z_rest, slice_mask[2], None, ALU.mult))
                settle()
                step(v.scalar_tensor_tensor(out=z_stack, in0=z_mid, scalar=slice_mask[1], in1=z_stack, op0=ALU.mult, op1=ALU.add))
                settle()
                v.scalar_tensor_tensor(out=z_stack, in0=z_hi, scalar=slice_mask[0], in1=z_stack,
                                       op0=ALU.mult, op1=ALU.add).then_inc(z_stacked, 1)

            Z_STEPS, PICK_STEPS = 6, 3

            def pick(tile, k, src):
                q = tile * PICKS + k
                b = k % 2
                s = src[:, 0:PICK_COLS].rearrange("p (b j) -> p b j", j=SPARSITY)
                h = hit[b].rearrange("p (b j) -> p b j", j=SPARSITY)
                r = rank[b].rearrange("p (b j) -> p b j", j=SPARSITY)
                dve.wait_ge(score_ready, q + 1)
                step(v.tensor_reduce(block_max[b], s, axis=AX.X, op=ALU.max))
                settle()
                v.tensor_tensor(h, s, block_max[b].unsqueeze(2).broadcast_to([P, PB, SPARSITY]), ALU.is_equal).then_inc(score_used, 1)
                dve.wait_ge(score_used, PICKS + q + 1)
                step(v.tensor_tensor(r, h, rev16[:, :].unsqueeze(1).broadcast_to([P, PB, SPARSITY]), ALU.mult))
                settle()
                step(v.tensor_reduce(winner[:, bass.ds(tile, 1), k * PB:(k + 1) * PB].rearrange("p a b -> p (a b)"), r,
                                     axis=AX.X, op=ALU.max))

            def w2_low(c0, c1):
                dve.wait_ge(w_scaled, 2)
                with dve.Fori(c0, c1) as c:
                    for k in range(2):
                        dve.wait_ge(w2_hi, c * 2 + (k + 1))
                        v.scalar_tensor_tensor(out=w2_part(c, k, 1)(0, H), in0=big32[:, bass.ds(c * W2_SLOT + (W2_AT + W2_SLOT + k * H), H)],
                                               scalar=w_scale[:, 1:2], in1=w2_part(c, k, 0)(0, H),
                                               op0=ALU.mult, op1=ALU.subtract).then_inc(w2_lo, 1)

            for u in range(3):
                for j in range(2):
                    swiglu(0, u, j)
                    if u:
                        i = 2 * (u - 1) + j
                        dve.wait_ge(w2_in[u - 1], 16)
                        quarter = C2 * W2_SLOT // 4
                        step(v.tensor_reduce(x_part[:, i:i + 1], w2_raw[:, i * quarter:(i + 1) * quarter], axis=AX.X,
                                             op=ALU.max, apply_absolute_value=True))
            settle()
            v.tensor_reduce(w_part[:, 2:3], x_part, axis=AX.X, op=ALU.max).then_inc(max_part, 1)
            dve.wait_ge(max_ready, len(MAX_ORDER))
            power_scales(w_all[:, 2:3], w_exp[:, 1:2], w_scale[:, 1:2], w_inv[:, 1:2], w_scaled)
            settle()
            step(v.scalar_tensor_tensor(out=hid_out, in0=w_inv[:, 1:2], scalar=2.0 ** 8, in1=w_inv[:, 1:2],
                                        op0=ALU.mult, op1=ALU.mult))
            for i in range(3):
                g, u, c = (3 + i) // U1, (3 + i) % U1, i * W2_UNIT
                swiglu(g, u, 0)
                w2_low(c, c + W2_FIRST)
                swiglu(g, u, 1)
                w2_low(c + W2_FIRST, min(c + W2_UNIT, C2))

            def unit1(g, u, tile, nxt=None):
                stack_z(tile, pick_b)
                pick(tile, 0, pick_a)
                swiglu(g, u, 0)
                pick(tile, 1, pick_b)
                if nxt is not None:
                    x1_low(nxt)
                pick(tile, 2, pick_a)
                swiglu(g, u, 1)
                pick(tile, 3, pick_b)

            TILE_STEPS = Z_STEPS + PICKS * PICK_STEPS

            def group1(g):
                moments(g - 1, 1)
                swiglu(g, 1, 0)
                normalise(g - 1, x1_ready)
                swiglu(g, 1, 1)
                x1_low(g * TPG - TPG)
                with steps.loop(2, U1, TILE_STEPS) as u:
                    unit1(g, u, (g - 1) * TPG + (u - 2), (g - 1) * TPG + (u - 1))

            dve.wait_ge(w2_lo, 2 * C2 + 2)
            take(0, down_ready, down_out[:, 0:1])
            with steps.loop(1, GROUPS - 1, NORM_STEPS + TPG * TILE_STEPS) as g:
                group1(g)
                unit1(g + 1, 0, g * TPG - 1)
                take(g, down_ready, down_out[:, bass.ds(g, 1)])
            group1(GROUPS - 1)

            def make_mask(g, u):
                if not (isinstance(g, int) and isinstance(u, int) and g == u == 0):
                    dve.wait_ge(hid_ready, (g * U2 + u) * 2)
                shape = [P, TPG, 2 * BPC, SPARSITY]
                v.tensor_tensor(mask.rearrange("p (t b j) -> p t b j", t=TPG, b=2 * BPC),
                                rev16[:, :].unsqueeze(1).unsqueeze(1).broadcast_to(shape),
                                winner[:, bass.ds(g * TPG, TPG), bass.ds(u * (2 * BPC), 2 * BPC)].unsqueeze(3).broadcast_to(shape),
                                ALU.not_equal).then_inc(mask_ready, 1)

            tile = (GROUPS - 1) * TPG - 1
            settle()
            dve.wait_ge(up_ready, N1)
            make_mask(0, 0)
            stack_z(tile, pick_b)
            for k in range(PICKS):
                pick(tile, k, pick_bank[k % 2])
            take(GROUPS - 1, down_ready, down_out[:, GROUPS - 1:GROUPS])

            def picked_units(g, norm):
                for i in range(2):
                    tile = g * 2 + ((GROUPS - 1) * TPG + i)
                    make_mask(g, 3 * i + 1)
                    if i == 0:
                        norm()
                    else:
                        pick(tile - 1, 3, pick_b)
                    x1_low(tile)
                    make_mask(g, 3 * i + 2)
                    stack_z(tile, pick_b)
                    pick(tile, 0, pick_a)
                    make_mask(g, 3 * i + 3)
                    pick(tile, 1, pick_b)
                    pick(tile, 2, pick_a)
                make_mask(g + 1, 0)
                pick(tile, 3, pick_b)
                take(g, sparse_ready, hid_out)

            def norm_phase1():
                moments(GROUPS - 1, 1)
                normalise(GROUPS - 1, x1_ready)

            def norm_phase2(g):
                moments(g, 2)
                normalise(g, rows_out)

            picked_units(0, norm_phase1)
            picked_units(1, lambda: norm_phase2(0))
            settle()
            for g in (2, 3):
                make_mask(g, 1)
                norm_phase2(g - 1)
                with dve.Fori(2, U2) as u:
                    make_mask(g, u)
                if g == 2:
                    make_mask(3, 0)
                    take(2, sparse_ready, hid_out)
            for t in range(TPG):
                take(3, sparse_ready, hid_out, [t])
                moments(3, 2, [t])
            normalise(3, rows_out)


INPUTS = ["x", "x_t", "ug_t", "point", "discount", "fuse_t", "w1_all", "c1_rep", "c2_rep", "w2_all", "consts"]


def constants():
    import numpy as np
    c = np.zeros((P, CONST_COLS), np.float32)
    for p in range(P):
        piece = p // RANK
        c[p, piece // 3] = 1
        c[p, 3 + piece % 3] = 1
    c[:, 6:6 + SPARSITY] = np.arange(SPARSITY, 0, -1)
    c[:, 6 + SPARSITY:] = np.eye(P)
    return c


def kernel(L0_attn_hidden_states, L0_attn_up_w, L0_attn_gate_w, L0_attn_local_point, L0_attn_local_approx_output,
           L0_attn_fuse_weight, L0_attn_discount_factor, L0_attn_ffn_gate_w, L0_attn_ffn_up_w, L0_attn_ffn_down_w,
           L0_ffn_c1_w, L0_ffn_c2_w, L0_ffn_w1, L0_ffn_w2t):
    import numpy as np
    import concourse.bacc as bacc
    from concourse import mybir as _mybir
    from concourse.bass_utils import run_bass_kernel_spmd

    a = np.asarray
    X = a(L0_attn_hidden_states).reshape(TOKENS, H)

    def chunks_first(w):
        return w.reshape(-1, P, KC, P).transpose(3, 0, 2, 1)

    def padded(w, axis):
        pad = [(0, 0), (0, 0)]
        pad[axis] = (0, C1 * P - F1)
        return np.pad(w, pad)

    gate, up = (chunks_first(padded(a(w), 0)).reshape(P, C1, H) for w in (L0_attn_ffn_gate_w, L0_attn_ffn_up_w))
    down = padded(a(L0_attn_ffn_down_w), 1).T.reshape(C1, P, H).transpose(1, 0, 2)
    w1 = chunks_first(a(L0_ffn_w1)).reshape(P, C2, H)
    w2 = a(L0_ffn_w2t).reshape(C2, P, H).transpose(1, 0, 2)
    fuse = np.concatenate([a(L0_attn_local_approx_output)[:, :, None], a(L0_attn_fuse_weight)], axis=2)
    ug = np.concatenate([a(L0_attn_up_w), a(L0_attn_gate_w)], axis=0)
    arrays = {
        "x": X,
        "x_t": X.T.reshape(KC, P, TOKENS).transpose(1, 0, 2),
        "ug_t": ug.T.reshape(KC, P, 2 * S).transpose(1, 0, 2).reshape(P, -1),
        "point": a(L0_attn_local_point).reshape(S, 1),
        "discount": np.tile(a(L0_attn_discount_factor).reshape(1, G), (P, 1)),
        "fuse_t": fuse.transpose(1, 2, 0).reshape(S, -1),
        "w1_all": np.stack([gate, up, down], axis=2).reshape(P, -1),
        "c1_rep": np.tile(a(L0_ffn_c1_w).T.reshape(KC, P, RANK).transpose(1, 0, 2), (1, 1, COPIES)).reshape(P, -1),
        "c2_rep": np.tile(a(L0_ffn_c2_w).T, (COPIES, 1)),
        "w2_all": np.stack([w1, w2], axis=2).reshape(P, -1),
        "consts": constants(),
    }
    arrays = {k: np.ascontiguousarray(v) for k, v in arrays.items()}
    nc = bacc.Bacc("TRN2", target_bir_lowering=False, num_devices=1)
    args = [nc.dram_tensor(f"in_{k}", arrays[k].shape, F32, kind="ExternalInput").ap() for k in INPUTS]
    args.append(nc.dram_tensor("out_0", (TOKENS, H), F32, kind="ExternalOutput").ap())
    program(nc, *args)
    r = run_bass_kernel_spmd(nc, [{f"in_{k}": v for k, v in arrays.items()}], core_ids=[0])
    return r.results[0]["out_0"].reshape(a(L0_attn_hidden_states).shape)
```
